# Optimizing a Trainium2 kernel written in Bass

```python
import numpy as np
import jax
import jax.numpy as jnp

def _softmax(x, axis=-1):
    return jax.nn.softmax(x, axis=axis)

def _gelu(x):
    return jax.nn.gelu(x, approximate=True)

def _silu(x):
    return jax.nn.silu(x)

def _sigmoid(x):
    return jax.nn.sigmoid(x)

def _layernorm(x, axis=-1, eps=1e-05):
    m = jnp.mean(x, axis=axis, keepdims=True)
    v = jnp.var(x, axis=axis, keepdims=True)
    return (x - m) / jnp.sqrt(v + eps)

def _scatter_add(tgt, idx, src, axis=0):
    return tgt.at[idx].add(src)

def _segment_sum(src, seg, n):
    return jax.ops.segment_sum(src, seg, n)
kernel_name = 'mk_lm_tower_d1_tok_ids2048_r4_105da2'

def setup_inputs(seed: int=0):
    np.random.seed(seed)
    _w = jnp.asarray

    def _rec_inputs():
        import jax
        import jax.numpy as jnp
        _rk = jax.random.key(seed)
        x = jax.random.randint(jax.random.fold_in(_rk, 1), (16, 512), 0, 12564, jnp.int32)
        return x
    x = _rec_inputs()

    def _L0_tok_setup():
        import jax, jax.numpy as jnp
        import numpy as np
        VOCAB = 50257
        EMBED_DIM = 512
        N_LAYERS = 2
        LOCAL_D = EMBED_DIM // 2 // N_LAYERS
        EMBD_D = EMBED_DIM - LOCAL_D * (2 * N_LAYERS - 1)
        KERNEL = 3
        B, T = (16, 512)

        def positional_encoding(max_len, d_model):
            depth = d_model // 2
            positions = jnp.arange(max_len, dtype=jnp.float32)[:, None]
            depths = jnp.arange(depth, dtype=jnp.float32)[None, :] / depth
            angle_rads = positions * (1.0 / 10000.0 ** depths)
            return jnp.concatenate([jnp.sin(angle_rads), jnp.cos(angle_rads)], axis=-1)

        def softpos_axis1(x, spos):
            n_subpos = spos.shape[0]
            m = x[:, :n_subpos, :]
            sel = jax.nn.softmax(m, axis=1)
            ext = jnp.einsum('bjt,jk->bkt', sel, spos)
            return jnp.concatenate([x, ext], axis=1)
        key = jax.random.key(seed)
        ks = jax.random.split(key, 6)
        return {'sequences': jax.random.randint(ks[0], (B, T), 0, VOCAB), 'emb_table': jax.random.normal(ks[1], (VOCAB, EMBD_D), dtype=jnp.float32), 'conv_w': jax.random.normal(ks[2], (LOCAL_D, EMBD_D, KERNEL), dtype=jnp.float32) * 0.05, 'conv_b': jax.random.normal(ks[3], (LOCAL_D,), dtype=jnp.float32) * 0.05, 'spos0': jax.random.normal(ks[4], (LOCAL_D, LOCAL_D), dtype=jnp.float32) * 0.05, 'spos1': jax.random.normal(ks[5], (LOCAL_D, LOCAL_D), dtype=jnp.float32) * 0.05}
    _L0_tok_all = _L0_tok_setup()
    _L0_tok_in = {k: v for k, v in _L0_tok_all.items() if k in ('emb_table', 'conv_w', 'conv_b', 'spos0', 'spos1')}
    del _L0_tok_all

    def _L0_attn_setup():
        import jax, jax.numpy as jnp
        import numpy as np
        HEADS = 16
        HIDDEN = 512
        HEAD_DIM = HIDDEN // HEADS
        key = jax.random.key(seed)
        ks = jax.random.split(key, 9)
        s = 1.0 / np.sqrt(HIDDEN)
        inp = {'x': jax.random.normal(ks[0], (2, 512, HIDDEN), dtype=jnp.float32)}
        for i, name in enumerate(['q', 'k', 'v', 'out']):
            inp[f'W{name}'] = jax.random.uniform(ks[1 + 2 * i], (HIDDEN, HIDDEN), minval=-s, maxval=s, dtype=jnp.float32)
            inp[f'b{name}'] = jax.random.uniform(ks[2 + 2 * i], (HIDDEN,), minval=-s, maxval=s, dtype=jnp.float32)
        return inp
    _L0_attn_all = _L0_attn_setup()
    _L0_attn_in = {k: v for k, v in _L0_attn_all.items() if k in ('Wq', 'bq', 'Wk', 'bk', 'Wv', 'bv', 'Wout', 'bout')}
    del _L0_attn_all

    def _L0_ffn_setup():
        import jax, jax.numpy as jnp
        import numpy as np
        D_MODEL = 512
        NUM_TILES = 64
        D_SLICE = D_MODEL // NUM_TILES
        TILES_PER_CLUSTER = 8
        NUM_CLUSTERS = NUM_TILES // TILES_PER_CLUSTER
        GRID = 16
        LN_EPS = 1e-05
        DIMS = (np.arange(NUM_TILES)[:, None] * D_SLICE + np.arange(D_SLICE)[None, :]) % D_MODEL
        DIMS = jnp.asarray(DIMS, dtype=jnp.int32)

        def _forward(x, ln_gamma, ln_beta, spline_bases, spline_slopes, output_scale):
            B, S, D = x.shape
            N = B * S
            mu = jnp.mean(x, axis=-1, keepdims=True)
            var = jnp.mean(jnp.square(x - mu), axis=-1, keepdims=True)
            xn = (x - mu) * jax.lax.rsqrt(var + LN_EPS) * ln_gamma + ln_beta
            xf = xn.reshape(N, D)
            slope_sign = jnp.sign(jnp.mean(spline_slopes, axis=-1))
            tile_sigs = jnp.zeros((NUM_TILES, D), dtype=x.dtype)
            tile_sigs = tile_sigs.at[jnp.arange(NUM_TILES)[:, None], DIMS].set(slope_sign)
            cluster_sigs = jnp.sign(tile_sigs.reshape(NUM_CLUSTERS, TILES_PER_CLUSTER, D).mean(axis=1))
            cluster_assign = jnp.arange(NUM_TILES, dtype=jnp.int32) // TILES_PER_CLUSTER
            input_sigs = jnp.sign(xf)
            cluster_scores = input_sigs @ cluster_sigs.T
            best_cluster = jnp.argmax(cluster_scores, axis=-1)
            tile_scores = input_sigs @ tile_sigs.T
            in_cluster = cluster_assign[None, :] == best_cluster[:, None]
            tile_idx = jnp.argmax(jnp.where(in_cluster, tile_scores, -jnp.inf), axis=-1)
            tok_dims = DIMS[tile_idx]
            x_slice = jnp.take_along_axis(xf, tok_dims, axis=1)
            tok_min = x_slice.min(axis=1)
            tok_max = x_slice.max(axis=1)
            onehot = tile_idx[None, :] == jnp.arange(NUM_TILES)[:, None]
            tile_min = jnp.where(onehot, tok_min[None, :], jnp.inf).min(axis=1)
            tile_max = jnp.where(onehot, tok_max[None, :], -jnp.inf).max(axis=1)
            mn = tile_min[tile_idx][:, None]
            mx = tile_max[tile_idx][:, None]
            u = jnp.clip((x_slice - mn) / (mx - mn + 1e-08), 0.0, 1.0 - 1e-06)
            gi = jnp.clip((u * GRID).astype(jnp.int32), 0, GRID - 1)
            j = jnp.arange(D_SLICE)[None, :]
            b = spline_bases[tile_idx[:, None], j, gi]
            s = spline_slopes[tile_idx[:, None], j, gi]
            x_local = (u - gi.astype(u.dtype) / GRID) * GRID
            delta = (b + s * x_local) * output_scale[tile_idx][:, None]
            out = jnp.zeros_like(xf).at[jnp.arange(N)[:, None], tok_dims].set(delta)
            return x + out.reshape(B, S, D)
        key = jax.random.key(seed)
        k1, k2, k3, k4, k5, k6 = jax.random.split(key, 6)
        x = jax.random.normal(k1, (4, 1024, D_MODEL), dtype=jnp.float32)
        ln_gamma = 1.0 + 0.1 * jax.random.normal(k2, (D_MODEL,), dtype=jnp.float32)
        ln_beta = 0.1 * jax.random.normal(k3, (D_MODEL,), dtype=jnp.float32)
        spline_bases = 0.1 * jax.random.normal(k4, (NUM_TILES, D_SLICE, GRID), dtype=jnp.float32)
        spline_slopes = 0.1 + 0.1 * jax.random.normal(k5, (NUM_TILES, D_SLICE, GRID), dtype=jnp.float32)
        output_scale = 1.0 + 0.1 * jax.random.normal(k6, (NUM_TILES,), dtype=jnp.float32)
        return {'x': x, 'ln_gamma': ln_gamma, 'ln_beta': ln_beta, 'spline_bases': spline_bases, 'spline_slopes': spline_slopes, 'output_scale': output_scale}
    _L0_ffn_all = _L0_ffn_setup()
    _L0_ffn_in = {k: v for k, v in _L0_ffn_all.items() if k in ('ln_gamma', 'ln_beta', 'spline_bases', 'spline_slopes', 'output_scale')}
    del _L0_ffn_all
    return {'x': x, 'L0_tok_emb_table': _L0_tok_in['emb_table'], 'L0_tok_conv_w': _L0_tok_in['conv_w'], 'L0_tok_conv_b': _L0_tok_in['conv_b'], 'L0_tok_spos0': _L0_tok_in['spos0'], 'L0_tok_spos1': _L0_tok_in['spos1'], 'L0_attn_Wq': _L0_attn_in['Wq'], 'L0_attn_bq': _L0_attn_in['bq'], 'L0_attn_Wk': _L0_attn_in['Wk'], 'L0_attn_bk': _L0_attn_in['bk'], 'L0_attn_Wv': _L0_attn_in['Wv'], 'L0_attn_bv': _L0_attn_in['bv'], 'L0_attn_Wout': _L0_attn_in['Wout'], 'L0_attn_bout': _L0_attn_in['bout'], 'L0_ffn_ln_gamma': _L0_ffn_in['ln_gamma'], 'L0_ffn_ln_beta': _L0_ffn_in['ln_beta'], 'L0_ffn_spline_bases': _L0_ffn_in['spline_bases'], 'L0_ffn_spline_slopes': _L0_ffn_in['spline_slopes'], 'L0_ffn_output_scale': _L0_ffn_in['output_scale']}

def reference(x, L0_tok_emb_table, L0_tok_conv_w, L0_tok_conv_b, L0_tok_spos0, L0_tok_spos1, L0_attn_Wq, L0_attn_bq, L0_attn_Wk, L0_attn_bk, L0_attn_Wv, L0_attn_bv, L0_attn_Wout, L0_attn_bout, L0_ffn_ln_gamma, L0_ffn_ln_beta, L0_ffn_spline_bases, L0_ffn_spline_slopes, L0_ffn_output_scale):
    import jax
    import jax.numpy as jnp

    def _L0_tok_ref(sequences, emb_table, conv_w, conv_b, spos0, spos1):
        import jax, jax.numpy as jnp
        import numpy as np
        VOCAB = 50257
        EMBED_DIM = 512
        N_LAYERS = 2
        LOCAL_D = EMBED_DIM // 2 // N_LAYERS
        EMBD_D = EMBED_DIM - LOCAL_D * (2 * N_LAYERS - 1)
        KERNEL = 3
        B, T = (16, 512)

        def positional_encoding(max_len, d_model):
            depth = d_model // 2
            positions = jnp.arange(max_len, dtype=jnp.float32)[:, None]
            depths = jnp.arange(depth, dtype=jnp.float32)[None, :] / depth
            angle_rads = positions * (1.0 / 10000.0 ** depths)
            return jnp.concatenate([jnp.sin(angle_rads), jnp.cos(angle_rads)], axis=-1)

        def softpos_axis1(x, spos):
            n_subpos = spos.shape[0]
            m = x[:, :n_subpos, :]
            sel = jax.nn.softmax(m, axis=1)
            ext = jnp.einsum('bjt,jk->bkt', sel, spos)
            return jnp.concatenate([x, ext], axis=1)
        seq_len = sequences.shape[1]
        x = emb_table[sequences] * jnp.sqrt(jnp.float32(EMBD_D))
        x = x + positional_encoding(seq_len, EMBD_D)[None]
        x = jnp.transpose(x, (0, 2, 1))
        dilation = 1
        x_pad = jnp.pad(x, ((0, 0), (0, 0), ((KERNEL - 1) * dilation, 0)))
        xc = jax.lax.conv_general_dilated(x_pad, conv_w, window_strides=(1,), padding='VALID', rhs_dilation=(dilation,), dimension_numbers=('NCH', 'OIH', 'NCH'))
        xc = xc + conv_b[None, :, None]
        y0 = softpos_axis1(x, spos0)
        y1 = softpos_axis1(xc, spos1)
        return jnp.concatenate([y0, y1], axis=1)

    def _L0_attn_ref(x, Wq, bq, Wk, bk, Wv, bv, Wout, bout):
        import jax, jax.numpy as jnp
        import numpy as np
        HEADS = 16
        HIDDEN = 512
        HEAD_DIM = HIDDEN // HEADS
        bsz, seq_len, _ = x.shape
        q = x @ Wq.T + bq
        k = x @ Wk.T + bk
        v = x @ Wv.T + bv
        q = q.reshape(bsz, seq_len, HEADS, HEAD_DIM).transpose(0, 2, 1, 3)
        k = k.reshape(bsz, seq_len, HEADS, HEAD_DIM).transpose(0, 2, 1, 3)
        v = v.reshape(bsz, seq_len, HEADS, HEAD_DIM).transpose(0, 2, 1, 3)
        scale = HEAD_DIM ** 0.5
        scores = jnp.einsum('bhqd,bhkd->bhqk', q, k) / scale
        weights = jax.nn.softmax(scores, axis=-1)
        attn = jnp.einsum('bhqk,bhkd->bhqd', weights, v)
        attn = attn.transpose(0, 2, 1, 3).reshape(bsz, seq_len, HIDDEN)
        return attn @ Wout.T + bout

    def _L0_ffn_ref(x, ln_gamma, ln_beta, spline_bases, spline_slopes, output_scale):
        import jax, jax.numpy as jnp
        import numpy as np
        D_MODEL = 512
        NUM_TILES = 64
        D_SLICE = D_MODEL // NUM_TILES
        TILES_PER_CLUSTER = 8
        NUM_CLUSTERS = NUM_TILES // TILES_PER_CLUSTER
        GRID = 16
        LN_EPS = 1e-05
        DIMS = (np.arange(NUM_TILES)[:, None] * D_SLICE + np.arange(D_SLICE)[None, :]) % D_MODEL
        DIMS = jnp.asarray(DIMS, dtype=jnp.int32)

        def _forward(x, ln_gamma, ln_beta, spline_bases, spline_slopes, output_scale):
            B, S, D = x.shape
            N = B * S
            mu = jnp.mean(x, axis=-1, keepdims=True)
            var = jnp.mean(jnp.square(x - mu), axis=-1, keepdims=True)
            xn = (x - mu) * jax.lax.rsqrt(var + LN_EPS) * ln_gamma + ln_beta
            xf = xn.reshape(N, D)
            slope_sign = jnp.sign(jnp.mean(spline_slopes, axis=-1))
            tile_sigs = jnp.zeros((NUM_TILES, D), dtype=x.dtype)
            tile_sigs = tile_sigs.at[jnp.arange(NUM_TILES)[:, None], DIMS].set(slope_sign)
            cluster_sigs = jnp.sign(tile_sigs.reshape(NUM_CLUSTERS, TILES_PER_CLUSTER, D).mean(axis=1))
            cluster_assign = jnp.arange(NUM_TILES, dtype=jnp.int32) // TILES_PER_CLUSTER
            input_sigs = jnp.sign(xf)
            cluster_scores = input_sigs @ cluster_sigs.T
            best_cluster = jnp.argmax(cluster_scores, axis=-1)
            tile_scores = input_sigs @ tile_sigs.T
            in_cluster = cluster_assign[None, :] == best_cluster[:, None]
            tile_idx = jnp.argmax(jnp.where(in_cluster, tile_scores, -jnp.inf), axis=-1)
            tok_dims = DIMS[tile_idx]
            x_slice = jnp.take_along_axis(xf, tok_dims, axis=1)
            tok_min = x_slice.min(axis=1)
            tok_max = x_slice.max(axis=1)
            onehot = tile_idx[None, :] == jnp.arange(NUM_TILES)[:, None]
            tile_min = jnp.where(onehot, tok_min[None, :], jnp.inf).min(axis=1)
            tile_max = jnp.where(onehot, tok_max[None, :], -jnp.inf).max(axis=1)
            mn = tile_min[tile_idx][:, None]
            mx = tile_max[tile_idx][:, None]
            u = jnp.clip((x_slice - mn) / (mx - mn + 1e-08), 0.0, 1.0 - 1e-06)
            gi = jnp.clip((u * GRID).astype(jnp.int32), 0, GRID - 1)
            j = jnp.arange(D_SLICE)[None, :]
            b = spline_bases[tile_idx[:, None], j, gi]
            s = spline_slopes[tile_idx[:, None], j, gi]
            x_local = (u - gi.astype(u.dtype) / GRID) * GRID
            delta = (b + s * x_local) * output_scale[tile_idx][:, None]
            out = jnp.zeros_like(xf).at[jnp.arange(N)[:, None], tok_dims].set(delta)
            return x + out.reshape(B, S, D)
        return _forward(x, ln_gamma, ln_beta, spline_bases, spline_slopes, output_scale)
    h = _L0_tok_ref(x, L0_tok_emb_table, L0_tok_conv_w, L0_tok_conv_b, L0_tok_spos0, L0_tok_spos1)
    h = h + _L0_attn_ref(_layernorm(h, axis=-1), L0_attn_Wq, L0_attn_bq, L0_attn_Wk, L0_attn_bk, L0_attn_Wv, L0_attn_bv, L0_attn_Wout, L0_attn_bout)
    h = h + _L0_ffn_ref(_layernorm(h, axis=-1), L0_ffn_ln_gamma, L0_ffn_ln_beta, L0_ffn_spline_bases, L0_ffn_spline_slopes, L0_ffn_output_scale)
    return h

_drawn_inputs = setup_inputs


def setup_inputs(seed=0):
    import zlib

    import numpy as np

    out = dict(_drawn_inputs(seed))
    spreads = {}
    factors = {'L0_tok_conv_b': 8.0,
     'L0_attn_Wq': 4.309,
     'L0_attn_bq': 8.0,
     'L0_attn_Wk': 4.322,
     'L0_attn_bk': 64.0,
     'L0_ffn_ln_gamma': 8.0,
     'L0_ffn_ln_beta': 8.0,
     'L0_ffn_spline_bases': 8.0,
     'L0_ffn_spline_slopes': 8.0,
     'L0_ffn_output_scale': 33.338}
    for name, (base, spread) in spreads.items():
        noise = np.random.default_rng([zlib.crc32(name.encode()), seed]).standard_normal(out[name].shape)
        drawn = base * np.exp(spread * noise) if base else spread * noise
        out[name] = jnp.asarray(drawn.astype(out[name].dtype))
    for name, factor in factors.items():
        out[name] = (out[name] * factor).astype(out[name].dtype)
    return out
```

```python
from contextlib import ExitStack

import numpy as np

import concourse.bass as bass
from concourse import mybir

F32 = mybir.dt.float32
F32R = mybir.dt.float32r
BF16 = mybir.dt.bfloat16
I32 = mybir.dt.int32
ALU = mybir.AluOpType
ACT = mybir.ActivationFunctionType
X_AXIS = mybir.AxisListType.X

P = 128
B = 16
T = 512
C = 128
R = 4
H, DH = 16, 32
G = 4
HG = H // G
KT = T // P
SLOTS = G * KT
NT = 64
DS = 8
CL = 8
GRID = 16
LN_EPS = 1e-5
BIG = 1e30
SCORE_ROWS = 3 * DH
SHIFT_ROWS = SCORE_ROWS + 2

UNITS = [
    [("V3", 0), ("EX", 1)],
    [("OUT0", -1), ("SEL0T", 1)],
    [("OUT1", -1), ("OUT2", -1), ("CONV", 1)],
    [("MT1", 0), ("OUT3", -1), ("EXT0", 1)],
    [("XCT", 1), ("Q3", 0)],
    [("K3", 0), ("SEL1T", 1)],
    [("EXT1", 1)],
    [("MT2", 0)],
    [("ZT0", 1), ("ZT1", 1)],
    [("ZT2", 1), ("ZT3", 1), ("Q0", 1)],
    [("K0", 1)],
    [("MT3", 0)],
    [("Q1", 1)],
    [("K1", 1), ("V0", 1)],
    [("Q2", 1), ("V1", 1)],
    [("MT0", 1), ("K2", 1), ("V2", 1)],
]
ORDER = [u for slot in UNITS for u in slot]
BANK = {name: k % 2 for k, (name, _) in enumerate(ORDER)}
OFFSET = dict(ORDER)

MAX_STEPS = [range(0, 6), range(6, 11), range(11, 16), range(16, 16)]

NORM_SLOT = [3, 5, 7, 9]
ROUTE_SLOT = [4, 6, 8, 10]
PICK_SLOT = [5, 7, 9, 11]

CONST_LOADS = 20
FRONT_STEPS = 5
LN1_STEPS = 6
LN2_STEPS = 19
CHOOSE_STEPS = 10
ROUTE_STEPS = 18


def run_batches(eng, batch):
    for b in range(-1, 2):
        batch(b)
    with eng.Fori(2, B - 2) as b:
        batch(b)
    for b in range(B - 2, B + 1):
        batch(b)


def present(n):
    return not isinstance(n, int) or 0 <= n < B


def wait(eng, sem, value):
    if isinstance(value, int) and value <= 0:
        return
    eng.wait_ge(sem, value)


def apart(eng, carrier):
    eng.sem_inc(carrier, 1)


def build(nc, io):
    with ExitStack() as ctx:
        def sb(name, shape, dt=F32):
            return ctx.enter_context(nc.sbuf_tensor(name, shape, dt))

        def ps(name, shape):
            return ctx.enter_context(nc.psum_tensor(name, shape, F32))

        def sem(name):
            return ctx.enter_context(nc.semaphore(name))

        q_stack = sb("q_stack", [P, G, HG, T], F32R)
        k_stack = sb("k_stack", [P, G, HG, T], F32R)
        wq = [sb(f"wq_{p}", [P, KT, T], F32R) for p in ("hi", "lo")]
        wk = [sb(f"wk_{p}", [P, KT, T], F32R) for p in ("hi", "lo")]
        wv = [sb(f"wv_{p}", [P, KT, T], F32R) for p in ("hi", "lo")]
        wo = sb("wo", [P, KT, T])
        z_t = [sb(f"z_t_{p}", [P, KT, T], F32R) for p in ("hi", "lo")]
        v = sb("v", [P, KT, T])
        prob = sb("prob", [P, HG, T])
        attn_t = sb("attn_t", [P, KT, T])
        back_h = sb("back_h", [P, R, T])
        h_emb = sb("h_emb", [P, 2 + T])
        h_rest = sb("h_rest", [P, R - 1, T])
        qk_part = [sb(f"qk_{p}", [P, 2, T], F32R) for p in ("hi", "lo")]
        recip = sb("recip", [P, T])
        emb = sb("emb", [P, KT, C])
        sel = sb("sel", [P, KT, C])
        sel_t = sb("sel_t", [P, T])
        posenc = sb("posenc", [P, KT, C])
        xf = sb("xf", [P, 2, T])
        sign = sb("sign", [P, 2, T], BF16)
        gamma = sb("gamma", [P, T])
        beta = sb("beta", [P, T])
        bout = sb("bout", [P, T])
        bv = sb("bv", [P, T])
        slope_sign = sb("slope_sign", [P, T], BF16)
        conv_w = sb("conv_w", [P, 3, C])
        conv_b = sb("conv_b", [P, 1])
        spos = sb("spos", [P, 2, C])
        ident = sb("ident", [P, P])
        ones = sb("ones", [P, P])
        bqk = sb("bqk", [P, 2, G])
        token_ids = sb("token_ids", [P, KT], I32)
        sel_stat = sb("sel_stat", [P, 4, KT])
        row_max = sb("row_max", [P, HG * KT])
        shift = sb("shift", [P, 2 * HG * KT], F32R)
        shift_t = sb("shift_t", [2 * HG * KT, P], F32R)
        stats1 = sb("stats1", [P, R, 6])
        mv1 = sb("mv1", [P, R, 2])
        rstd1 = sb("rstd1", [P, R])
        scr1 = sb("scr1", [P, 2, R])
        stats2 = sb("stats2", [P, R, 6])
        mv2 = sb("mv2", [P, R, 2])
        coef = sb("coef", [P, R, 4])
        scr2 = sb("scr2", [P, 8])
        expo = sb("expo", [P, R])
        tile_score = sb("tile_score", [P, NT])
        cluster_score = sb("cluster_score", [P, CL])
        cluster_key = sb("cluster_key", [P, CL])
        tile_key = sb("tile_key", [P, NT])
        key = sb("key", [P, NT])
        key_max = sb("key_max", [P, 1])
        onehot = sb("onehot", [P, 2, NT])
        picked = sb("picked", [P, NT])
        off_mask = sb("off_mask", [P, NT])
        cand = sb("cand", [P, NT])
        tok_ext = sb("tok_ext", [P, 2])
        tile_max = sb("tile_max", [P, NT])
        tile_min = sb("tile_min", [P, NT])
        iota_tile = sb("iota_tile", [P, NT])
        tile_tie = sb("tile_tie", [P, NT])
        cluster_tie = sb("cluster_tie", [P, CL])
        iota_grid = sb("iota_grid", [P, GRID])
        row_base = sb("row_base", [P, B, R])
        tile_idx = sb("tile_idx", [P, B, R])
        slices = sb("slices", [P, B, R, DS])
        table = sb("table", [NT, 2 * DS * GRID + 3])
        mean_slope = sb("mean_slope", [NT, DS])
        tile_sign = sb("tile_sign", [NT, DS])

        def onehots(n):
            return xf[:, n % 2, 0:R * NT].rearrange("p (r t) -> p r t", t=NT)

        def onehot_t4(n):
            return (prob, v, attn_t, back_h)[n // 4][0:NT, n % 4, :]

        def onehot_t(n, r):
            return onehot_t4(n)[:, r * P:(r + 1) * P]

        def by_token(buf):
            return buf.rearrange("p a b -> p (a b)").rearrange("p (k j) -> p k j", j=DS)

        def grids(buf):
            return buf.rearrange("p (r j g) -> p r j g", r=R, j=DS)

        tok = gamma[:, 0:3 * B * R].rearrange("p (c k) -> p c k", c=3)
        span = gamma[:, 3 * B * R:4 * B * R]
        place = beta[:, 0:B * R].bitcast(I32).rearrange("p (b r) -> p b r", r=R)
        grid_val = bv[:, 0:R * DS].rearrange("p (r j) -> p r j", j=DS)
        cell, above, cell_int = by_token(sel[:, :, :]), by_token(emb[:, :, :]), by_token(posenc[:, :, :].bitcast(I32))
        delta = sel_t[:, :].rearrange("p (b r j) -> p b r j", b=B, r=R)

        def work(n):
            return grids(h_rest[:, n % 2, :])

        def mask(n):
            return grids(recip[:, :] if n % 2 else h_rest[:, 2, :])

        ps_t = ps("ps_t", [P, 2, T])
        ps_m = ps("ps_m", [P, 2, T])
        ps_u = ps("ps_u", [P, 2, T])
        ps_v = ps("ps_v", [P, T])
        ps_s = ps("ps_s", [P, T])

        const_in = sem("const_in")
        weight_in = sem("weight_in")
        weight_hi = sem("weight_hi")
        weight_lo = sem("weight_lo")
        setup_vec = sem("setup_vec")
        sign_row = sem("sign_row")
        sign_bcast = sem("sign_bcast")
        ids_in = sem("ids_in")
        rows_in = sem("rows_in")
        emb_ready = sem("emb_ready")
        front_mm = sem("front_mm")
        h_emb_ready = sem("h_emb_ready")
        conv_ready = sem("conv_ready")
        ext_ready = sem("ext_ready")
        sel_max = sem("sel_max")
        sel_exp = sem("sel_exp")
        sel_ready = sem("sel_ready")
        sel_t_ready = sem("sel_t_ready")
        spilled = sem("spilled")
        front_vec = sem("front_vec")
        ln1_stats = sem("ln1_stats")
        ln1_pool = sem("ln1_pool")
        z_ready = sem("z_ready")
        z_mm = sem("z_mm")
        z_hi = sem("z_hi")
        z_lo = sem("z_lo")
        q_mm = sem("q_mm")
        k_mm = sem("k_mm")
        v_mm = sem("v_mm")
        v_ready = sem("v_ready")
        qk_hi_ready = sem("qk_hi_ready")
        qk_lo_ready = sem("qk_lo_ready")
        stack_hi = sem("stack_hi")
        stack_in = sem("stack_in")
        max_mm = sem("max_mm")
        max_ready = sem("max_ready")
        shift_ready = sem("shift_ready")
        shift_mm = sem("shift_mm")
        shift_t_ready = sem("shift_t_ready")
        shift_in = sem("shift_in")
        score_mm = sem("score_mm")
        prob_ready = sem("prob_ready")
        attn_mm = sem("attn_mm")
        recip_ready = sem("recip_ready")
        attn_ready = sem("attn_ready")
        out_mm = sem("out_mm")
        back_in = sem("back_in")
        bout_added = sem("bout_added")
        h2_ready = sem("h2_ready")
        ln2_stats = sem("ln2_stats")
        ln2_pool = sem("ln2_pool")
        xn_ready = sem("xn_ready")
        xg_ready = sem("xg_ready")
        xf_ready = sem("xf_ready")
        base_ready = sem("base_ready")
        base_out = sem("base_out")
        sign_ready = sem("sign_ready")
        route_vec = sem("route_vec")
        masked = sem("masked")
        dve_carrier = sem("dve_carrier")
        pool_carrier = sem("pool_carrier")
        sync_carrier = sem("sync_carrier")
        fin_vec = sem("fin_vec")
        fin_pe = sem("fin_pe")
        fin_act = sem("fin_act")
        fin_delta = sem("fin_delta")
        scattered = sem("scattered")

        freed = {"EX": (h_emb_ready, 1, 1), "SEL0T": (sel_t_ready, 2, 1), "CONV": (conv_ready, 1, 1),
                 "EXT0": (ext_ready, 2, 1), "XCT": (sel_exp, 2, 2), "SEL1T": (sel_t_ready, 2, 2),
                 "EXT1": (ext_ready, 2, 2)}
        for j in range(4):
            freed[f"ZT{j}"] = (z_lo, 4, j + 1)
            freed[f"Q{j}"] = (qk_lo_ready, 8, 2 * j + 1)
            freed[f"K{j}"] = (qk_lo_ready, 8, 2 * j + 2)
            freed[f"V{j}"] = (v_ready, 4, j + 1)
            freed[f"OUT{j}"] = (h2_ready, 4, j + 1)
            freed[f"MT{j}"] = (shift_t_ready, 4, j + 1)

        def wait_bank(pe, b, name):
            at = [n for n, _ in ORDER].index(name)
            for back in range(1, 3 * len(ORDER)):
                k = at - back
                turn, k = k // len(ORDER), k % len(ORDER)
                before, offset = ORDER[k]
                if BANK[before] == BANK[name] and present(b + turn + offset):
                    s, per, within = freed[before]
                    wait(pe, s, (b + turn + offset) * per + within)
                    return

        def unit_bank(name):
            return ps_u[:, BANK[name], :]

        def h_tile(r):
            return h_emb[:, 2:2 + T] if r == 0 else h_rest[:, r - 1, :]

        def next_group(b, g):
            return (b, g + 1) if g < G - 1 else (b + 1, 0)

        def group_before(b, g):
            return (b, g - 1) if g > 0 else (b - 1, G - 1)

        out_rows = io["out"].rearrange("b (r p) t -> b r p t", p=P)
        x_ids = io["x"].rearrange("b (p t) -> b p t", t=KT)

        block = ctx.enter_context(nc.Block())

        @block.sync
        def _(sp):
            weights = [(prob, "WqT"), (v, "WkT"), (attn_t, "WvT"), (wo, "WoT")]
            loads = [(posenc[:, :, :], io["posenc"].rearrange("(p t) c -> p t c", t=KT)),
                     (ident[:, :], io["ident"]),
                     (gamma[:, :], io["gamma"].partition_broadcast(P)), (beta[:, :], io["beta"].partition_broadcast(P)),
                     (bout[:, :], io["bout"].partition_broadcast(P)), (bv[:, :], io["bv"].partition_broadcast(P)),
                     (conv_w[:, :, :], io["conv_w"].rearrange("k i o -> i k o")),
                     (conv_b[:, :], io["conv_b"].rearrange("(p o) -> p o", o=1)),
                     (spos[:, 0, :], io["spos0"]), (spos[:, 1, :], io["spos1"]),
                     (bqk[:, 0, :], io["bq"]), (bqk[:, 1, :], io["bk"]),
                     (iota_tile[:, :], io["iota_tile"].partition_broadcast(P)),
                     (tile_tie[:, :], io["tile_tie"].partition_broadcast(P)),
                     (cluster_tie[:, :], io["cluster_tie"].partition_broadcast(P)),
                     (iota_grid[:, :], io["iota_grid"].partition_broadcast(P)),
                     (row_base[:, :, :], io["row_base"]),
                     (table[:, 0:128], io["bases"].rearrange("t j g -> t (j g)")),
                     (table[:, 128:256], io["slopes"].rearrange("t j g -> t (j g)")),
                     (table[:, 256:257], io["oscale"].rearrange("(t o) -> t o", o=1))]
            assert len(loads) == CONST_LOADS
            sp.dma_start(token_ids[:, :], x_ids[0]).then_inc(ids_in, 16)
            for dst, src in loads:
                sp.dma_start(dst, src).then_inc(const_in, 16)
            for dst, name in weights:
                sp.dma_start(dst[:, :, :], io[name].rearrange("(c p) n -> p c n", p=P)).then_inc(weight_in, 16)
            sp.wait_ge(setup_vec, 5)
            sp.dma_start(recip[0:1, :].rearrange("o (t j) -> o t j", j=DS), tile_sign[:, :]).then_inc(sign_row, 16)

            def spill(n, r):
                sp.dma_start(out_rows[n, r], h_tile(r)).then_inc(spilled, 16)

            def to_stack(n, g, which):
                k = n * 8 + 2 * g + which
                stack = (k_stack if which else q_stack)[:, :, :, :].bitcast(F32)
                hi, lo = (qk_part[p][:, which, :].bitcast(F32) for p in (0, 1))
                again, low = (DH, 2 * DH) if which else (2 * DH, DH)
                wait(sp, stack_in, 80 * k)
                apart(sp, sync_carrier)
                sp.wait_ge(qk_hi_ready, k + 1)
                for i in range(HG):
                    sp.dma_start(stack[0:DH, g, i, :], hi[DH * i:DH * (i + 1), :]).then_inc(stack_hi, 16)
                sp.wait_ge(qk_lo_ready, k + 1)
                for i in range(HG):
                    sp.dma_start(stack[low:low + DH, g, i, :], lo[DH * i:DH * (i + 1), :]).then_inc(stack_in, 16)
                sp.wait_ge(stack_hi, 64 * (k + 1))
                apart(sp, sync_carrier)
                sp.dma_start(stack[again:again + DH, g, :, :], stack[0:DH, g, :, :]).then_inc(stack_in, 16)

            def shift_rows(n, g):
                sp.wait_ge(shift_t_ready, n * G + g + 1)
                for part in range(2):
                    row = SCORE_ROWS + part
                    sp.dma_start(q_stack[row:row + 1, g, :, :].bitcast(F32).rearrange("o i (q c) -> o (i q) c", c=P),
                                 shift_t[part * 16:part * 16 + 16, :].bitcast(F32)).then_inc(shift_in, 16)

            def batch(b):
                for t in range(SLOTS):
                    for name, offset in UNITS[t]:
                        n = b + offset
                        if not present(n):
                            continue
                        if name == "EX":
                            sp.wait_ge(h_emb_ready, n + 1)
                            spill(n, 0)
                        elif name in ("EXT0", "EXT1"):
                            which = int(name[-1])
                            sp.wait_ge(ext_ready, 2 * n + which + 1)
                            spill(n, 2 * which + 1)
                        elif name == "CONV":
                            sp.wait_ge(conv_ready, n + 1)
                            spill(n, 2)
                        elif name[0] in "QK":
                            to_stack(n, int(name[1]), "QK".index(name[0]))
                        elif name[:2] == "MT":
                            shift_rows(n, int(name[2]))
                    if t in NORM_SLOT and present(b - 1):
                        n, r = b - 1, NORM_SLOT.index(t)
                        sp.wait_ge(base_ready, n * R + r + 1)
                        apart(sp, sync_carrier)
                        sp.dma_start(out_rows[n, r], back_h[:, r, :]).then_inc(base_out, 16)
                    if t == 4 and present(b + 2):
                        sp.wait_ge(rows_in, 64 * (b + 2))
                        apart(sp, sync_carrier)
                        sp.dma_start(token_ids[:, :], x_ids[b + 2]).then_inc(ids_in, 16)
                    if t == 13 and present(b):
                        sp.wait_ge(spilled, 64 * (b + 1))
                        apart(sp, sync_carrier)
                        wait(sp, base_out, 64 * b)
                        apart(sp, sync_carrier)
                        for r in range(R):
                            sp.dma_start(back_h[:, r, :], out_rows[b, r]).then_inc(back_in, 16)

            run_batches(sp, batch)
            sp.wait_ge(spilled, 64 * B)
            sp.wait_ge(base_out, 64 * B)
            sp.wait_ge(scattered, 16 * B * R)

        @block.tensor
        def _(pe):
            mm = nc.tensor.matmul

            def transposes(out, ins, n_cols=P):
                for j, a in enumerate(ins):
                    last = nc.tensor.transpose(out[:, j * n_cols:(j + 1) * n_cols], a, ident[:, :])
                return last

            def product3(out, lhs, rhs):
                for c in range(KT):
                    for a, w in ((0, 0), (1, 0), (0, 1)):
                        last = mm(out, lhs(a, c), rhs(w, c), start=(c == 0 and a == w), stop=(c == KT - 1 and w == 1))
                return last

            def unit(b, name, n):
                bank = unit_bank(name)
                j = int(name[-1]) if name[-1].isdigit() else 0
                if name == "EX":
                    pe.wait_ge(emb_ready, n + 1)
                elif name in ("SEL0T", "SEL1T"):
                    j = int(name[3])
                    pe.wait_ge(sel_ready, 2 * n + j + 1)
                elif name == "CONV":
                    pe.wait_ge(h_emb_ready, n + 1)
                elif name[:3] == "EXT":
                    pe.wait_ge(sel_t_ready, 2 * n + j + 1)
                elif name == "XCT":
                    pe.wait_ge(conv_ready, n + 1)
                elif name[:2] == "ZT":
                    pe.wait_ge(z_ready, R * n + R)
                elif name[0] in "QKV":
                    pe.wait_ge(z_lo, KT * n + KT)
                elif name[:3] == "OUT":
                    pe.wait_ge(attn_ready, G * n + G)
                elif name[:2] == "MT":
                    pe.wait_ge(shift_ready, 2 * (G * n + j) + 2)
                wait_bank(pe, b, name)
                if name == "EX":
                    transposes(bank, [emb[:, t, :] for t in range(KT)]).then_inc(front_mm, 1)
                elif name in ("SEL0T", "SEL1T"):
                    transposes(bank, [sel[:, t, :] for t in range(KT)]).then_inc(front_mm, 1)
                elif name == "CONV":
                    for k in range(3):
                        last = mm(bank, conv_w[:, k, :], h_emb[:, k:k + T], start=(k == 0), stop=(k == 2))
                    last.then_inc(front_mm, 1)
                elif name[:3] == "EXT":
                    mm(bank, spos[:, j, :], sel_t[:, :], start=True, stop=True).then_inc(front_mm, 1)
                elif name == "XCT":
                    transposes(bank, [h_rest[:, 1, t * P:(t + 1) * P] for t in range(KT)]).then_inc(front_mm, 1)
                elif name[:2] == "ZT":
                    transposes(bank, [h_tile(r)[:, j * P:(j + 1) * P] for r in range(R)]).then_inc(z_mm, 1)
                elif name[0] in "QK":
                    w, done = (wq, q_mm) if name[0] == "Q" else (wk, k_mm)
                    product3(bank, lambda a, c: w[a][:, c, j * P:(j + 1) * P],
                             lambda a, c: z_t[a][:, c, :]).then_inc(done, 1)
                elif name[0] == "V":
                    product3(bank, lambda a, c: z_t[a][:, c, j * P:(j + 1) * P],
                             lambda a, c: wv[a][:, c, :]).then_inc(v_mm, 1)
                elif name[:3] == "OUT":
                    for c in range(KT):
                        last = mm(bank, attn_t[:, c, j * P:(j + 1) * P], wo[:, c, :], start=(c == 0), stop=(c == KT - 1))
                    last.then_inc(out_mm, 1)
                elif name[:2] == "MT":
                    nc.tensor.transpose(bank[0:2 * HG * KT, 0:P], shift[:, :].bitcast(F32), ident[:, :]).then_inc(shift_mm, 1)

            def batch(b):
                for t in range(SLOTS):
                    g, kt = divmod(t, KT)
                    mn, mg = next_group(b, g)

                    def max_scores(steps):
                        for s in steps if present(mn) else ():
                            i, qt = divmod(s, KT)
                            if s == 0:
                                pe.wait_ge(stack_in, 80 * (8 * mn + 2 * mg + 2))
                            wait(pe, max_ready, 64 * mn + 16 * mg + s - 1)
                            mm(ps_m[:, s % 2, :], q_stack[0:SCORE_ROWS, mg, i, qt * P:(qt + 1) * P],
                               k_stack[0:SCORE_ROWS, mg, i, :], start=True, stop=True).then_inc(max_mm, 1)

                    def scores(heads):
                        for i in heads if present(b) else ():
                            if kt == 0 and i == 0:
                                pe.wait_ge(shift_in, 32 * (G * b + g + 1))
                            wait(pe, prob_ready, 64 * b + 16 * g + 4 * kt + i - 1)
                            mm(ps_t[:, i % 2, :], k_stack[0:SHIFT_ROWS, g, i, kt * P:(kt + 1) * P],
                               q_stack[0:SHIFT_ROWS, g, i, :], start=True, stop=True).then_inc(score_mm, 1)

                    steps = list(MAX_STEPS[kt])
                    half = (len(steps) + 1) // 2
                    scores((0, 1))
                    max_scores(steps[:half])
                    scores((2, 3))
                    max_scores(steps[half:])
                    for name, offset in UNITS[t]:
                        if present(b + offset):
                            unit(b, name, b + offset)
                    if present(b):
                        pe.wait_ge(prob_ready, 64 * b + 16 * g + 4 * kt + 4)
                        if g == 0:
                            pe.wait_ge(v_ready, KT * b + kt + 1)
                        if kt == 0:
                            wait(pe, attn_ready, G * b + g)
                        for i in range(HG):
                            hh = HG * g + i
                            mm(ps_v[DH * i:DH * (i + 1), :], v[:, kt, DH * hh:DH * (hh + 1)], prob[:, i, :],
                               start=(kt == 0), stop=(kt == KT - 1))
                        for i in range(HG):
                            last = mm(ps_s[DH * i:DH * (i + 1), :], ones[:, 0:DH], prob[:, i, :],
                                      start=(kt == 0), stop=(kt == KT - 1))
                        last.then_inc(attn_mm, 1)

            pe.wait_ge(sign_row, 16)
            pe.wait_ge(setup_vec, 2)
            mm(unit_bank("V3"), ones[0:1, :], recip[0:1, :], start=True, stop=True).then_inc(sign_bcast, 1)
            pe.wait_ge(setup_vec, 6)
            pe.wait_ge(const_in, 16 * CONST_LOADS)
            pe.wait_ge(weight_in, 16 * 4)
            pe.wait_ge(weight_lo, 3)
            run_batches(pe, batch)

            pe.wait_ge(route_vec, ROUTE_STEPS * R * B)
            nc.tensor.transpose(ps_m[0:NT, 0, 0:P], tile_max[:, :], ident[:, :])
            nc.tensor.transpose(ps_m[0:NT, 1, 0:P], tile_min[:, :], ident[:, :]).then_inc(fin_pe, 1)
            for n in range(B):
                pe.wait_ge(fin_vec, 1 + n)
                if n >= 2:
                    pe.wait_ge(fin_act, n - 1)
                for r in range(R):
                    last = nc.tensor.transpose(ps_u[0:NT, n % 2, r * P:(r + 1) * P], onehots(n)[:, r, :], ident[:, :])
                last.then_inc(fin_pe, 1)
            pe.wait_ge(fin_vec, 1 + B)
            for n in range(B):
                pe.wait_ge(fin_act, n + 1)
                for r in range(R):
                    k = 3 * (n * R + r)
                    last = mm(ps_s[:, k:k + 3], onehot_t(n, r), table[:, 256:259], start=True, stop=True)
            last.then_inc(fin_pe, 1)
            for n in range(B):
                pair = (ps_t, ps_m)[n % 2]
                if n >= 2:
                    pe.wait_ge(fin_delta, n - 1)
                for r in range(R):
                    last = mm(pair[:, r // 2, (r % 2) * 256:(r % 2) * 256 + 256], onehot_t(n, r), table[:, 0:256],
                              start=True, stop=True)
                last.then_inc(fin_pe, 1)

        @block.scalar
        def _(act):
            a = nc.scalar.activation
            for k, (src, dst) in enumerate(((prob, wq), (v, wk), (attn_t, wv))):
                act.wait_ge(weight_in, 16 * 4)
                a(dst[0][:, :, :], src[:, :, :], ACT.Copy).then_inc(weight_hi, 1)
            act.wait_ge(const_in, 16 * CONST_LOADS)

            def sel_exps(n, which, src):
                act.wait_ge(sel_max, 2 * n + which + 1)
                wait(act, front_mm, 7 * n + (2 if which else -1))
                for t in range(KT):
                    last = a(sel[:, t, :], src[:, t, :], ACT.Exp, bias=sel_stat[:, 1, t:t + 1],
                             accum_out=sel_stat[:, 2, t:t + 1])
                last.then_inc(sel_exp, 1)

            def unit(b, name, n):
                bank = unit_bank(name)
                j = int(name[-1]) if name[-1].isdigit() else 0
                if name == "EX":
                    act.wait_ge(front_mm, 7 * n + 1)
                    wait(act, z_mm, KT * n)
                    a(h_emb[:, 2:2 + T].rearrange("c (p t) -> c t p", t=KT),
                      bank.rearrange("c (t p) -> c t p", t=KT), ACT.Copy).then_inc(h_emb_ready, 1)
                    sel_exps(n, 0, emb)
                elif name == "XCT":
                    act.wait_ge(front_mm, 7 * n + 5)
                    sel_exps(n, 1, bank.rearrange("p (t c) -> p t c", t=KT))
                elif name in ("SEL0T", "SEL1T"):
                    j = int(name[3])
                    act.wait_ge(front_mm, 7 * n + (6 if j else 2))
                    wait(act, front_mm, 7 * n + (4 if j else 0))
                    a(sel_t[:, :], bank, ACT.Copy).then_inc(sel_t_ready, 1)
                elif name == "CONV":
                    act.wait_ge(front_mm, 7 * n + 3)
                    wait(act, z_mm, KT * n)
                    a(h_rest[:, 1, :], bank, ACT.Identity, bias=conv_b[:, 0:1]).then_inc(conv_ready, 1)
                elif name[:2] == "ZT":
                    act.wait_ge(z_mm, KT * n + j + 1)
                    wait(act, k_mm, G * n)
                    wait(act, v_mm, KT * n)
                    a(z_t[0][:, j, :], bank, ACT.Copy).then_inc(z_hi, 1)
                elif name[0] in "QK":
                    which = "QK".index(name[0])
                    act.wait_ge((q_mm, k_mm)[which], G * n + j + 1)
                    wait(act, stack_in, 80 * (8 * n + 2 * j + which - 1))
                    a(qk_part[0][:, which, :], bank, ACT.Identity, bias=bqk[:, which, j:j + 1]).then_inc(qk_hi_ready, 1)
                elif name[:2] == "MT":
                    act.wait_ge(shift_mm, G * n + j + 1)
                    wait(act, shift_in, 32 * (G * n + j))
                    a(shift_t[:, :], bank[0:2 * HG * KT, 0:P], ACT.Copy).then_inc(shift_t_ready, 1)

            def batch(b):
                for t in range(SLOTS):
                    for i in range(HG) if present(b) else ():
                        s = 64 * b + 4 * t + i
                        act.wait_ge(score_mm, s + 1)
                        if i == 0:
                            wait(act, attn_mm, 16 * b + t)
                        a(prob[:, i, :], ps_t[:, i % 2, :], ACT.Exp, scale=float(DH) ** -0.5).then_inc(prob_ready, 1)
                    for name, offset in UNITS[t]:
                        if present(b + offset):
                            unit(b, name, b + offset)
                    n = b - 1
                    if present(n) and t in NORM_SLOT:
                        r = NORM_SLOT.index(t)
                        act.wait_ge(ln2_pool, LN2_STEPS * (R * n + r + 1))
                        wait(act, route_vec, ROUTE_STEPS * (R * n + r - 2) + CHOOSE_STEPS + 1)
                        a(xf[:, r % 2, :], back_h[:, r, :], ACT.Identity, bias=coef[:, r, 3:4],
                          scale=coef[:, r, 2:3]).then_inc(xn_ready, 1)
                    if present(n) and t in ROUTE_SLOT:
                        r = ROUTE_SLOT.index(t)
                        act.wait_ge(xf_ready, R * n + r + 1)
                        wait(act, route_vec, ROUTE_STEPS * (R * n + r - 2) + 2)
                        a(sign[:, r % 2, :], xf[:, r % 2, :], ACT.Sign).then_inc(sign_ready, 1)

            run_batches(act, batch)
            act.wait_ge(base_out, 64 * B)
            for n in range(B):
                act.wait_ge(fin_pe, 2 + n)
                a(onehot_t4(n), ps_u[0:NT, n % 2, :], ACT.Copy).then_inc(fin_act, 1)

        @block.vector
        def _(dve):
            vec = nc.vector
            vec.memset(k_stack[SCORE_ROWS:P, :, :, :].bitcast(F32), 1.0).then_inc(setup_vec, 1)
            vec.memset(ones[:, :], 1.0)
            vec.memset(h_emb[:, 0:2], 0.0)
            vec.memset(expo[:, :], -0.5)
            vec.memset(tile_max[:, :], -BIG)
            vec.memset(tile_min[:, :], BIG).then_inc(setup_vec, 1)
            dve.wait_ge(const_in, 16 * CONST_LOADS)
            vec.reduce_sum(mean_slope[:, :], table[:, 128:256].rearrange("t (j g) -> t j g", g=GRID), X_AXIS).then_inc(setup_vec, 1)
            dve.wait_ge(setup_vec, 3)
            vec.tensor_scalar(tile_sign[:, :], mean_slope[:, :], 0.0, None, ALU.is_lt).then_inc(setup_vec, 1)
            dve.wait_ge(setup_vec, 4)
            vec.scalar_tensor_tensor(tile_sign[:, :], mean_slope[:, :], 0.0, tile_sign[:, :],
                                     ALU.is_gt, ALU.subtract).then_inc(setup_vec, 1)
            dve.wait_ge(sign_bcast, 1)
            vec.tensor_copy(slope_sign[:, :], unit_bank("V3")).then_inc(setup_vec, 1)
            for k, (src, dst) in enumerate(((prob, wq), (v, wk), (attn_t, wv))):
                dve.wait_ge(weight_hi, k + 1)
                vec.tensor_tensor(dst[1][:, :, :], src[:, :, :], dst[0][:, :, :].bitcast(F32), ALU.subtract).then_inc(weight_lo, 1)
            dve.wait_ge(weight_lo, 3)

            def embed(n):
                dve.wait_ge(rows_in, 64 * (n + 1))
                vec.scalar_tensor_tensor(emb[:, :, :], emb[:, :, :], float(np.sqrt(np.float32(C))), posenc[:, :, :],
                                         ALU.mult, ALU.add).then_inc(emb_ready, 1)

            def chain(n, k, ins):
                ins.then_inc(front_vec, 1)
                dve.wait_ge(front_vec, FRONT_STEPS * n + k)

            def selection_max(n, which, src):
                chain(n, 2 * which + 1, vec.reduce_max(sel_stat[:, 0, :], src, X_AXIS))
                ins = vec.tensor_scalar(sel_stat[:, 1, :], sel_stat[:, 0, :], -1.0, None, ALU.mult)
                ins.then_inc(sel_max, 1)

            def selection_norm(n, which):
                dve.wait_ge(sel_exp, 2 * n + which + 1)
                chain(n, 2 * which + 2, vec.reciprocal(sel_stat[:, 3, :], sel_stat[:, 2, :]))
                vec.tensor_tensor(sel[:, :, :], sel[:, :, :], sel_stat[:, 3, :].unsqueeze(2).to_broadcast([P, KT, C]),
                                  ALU.mult).then_inc(sel_ready, 1)

            def unit(b, name, n):
                bank = unit_bank(name)
                j = int(name[-1]) if name[-1].isdigit() else 0
                if name == "EX":
                    dve.wait_ge(emb_ready, n + 1)
                    selection_max(n, 0, emb[:, :, :])
                elif name == "XCT":
                    dve.wait_ge(front_mm, 7 * n + 5)
                    selection_max(n, 1, bank.rearrange("p (t c) -> p t c", t=KT))
                elif name[:3] == "EXT":
                    dve.wait_ge(front_mm, 7 * n + (7 if j else 4))
                    wait(dve, z_mm, KT * n)
                    out = h_rest[:, 2 * j, :]
                    if j == 0:
                        out, bank = out.rearrange("c (p t) -> c t p", t=KT), bank.rearrange("c (t p) -> c t p", t=KT)
                    vec.tensor_copy(out, bank).then_inc(ext_ready, 1)
                elif name[:2] == "ZT":
                    dve.wait_ge(z_hi, KT * n + j + 1)
                    vec.tensor_tensor(z_t[1][:, j, :], bank, z_t[0][:, j, :].bitcast(F32), ALU.subtract).then_inc(z_lo, 1)
                elif name[0] in "QK":
                    which = "QK".index(name[0])
                    dve.wait_ge(qk_hi_ready, 8 * n + 2 * j + which + 1)
                    vec.scalar_tensor_tensor(qk_part[1][:, which, :], bank, bqk[:, which, j:j + 1],
                                             qk_part[0][:, which, :].bitcast(F32), ALU.add, ALU.subtract).then_inc(qk_lo_ready, 1)
                elif name[0] == "V":
                    dve.wait_ge(v_mm, KT * n + j + 1)
                    wait(dve, attn_mm, 16 * (n - 1) + 12 + j + 1)
                    vec.tensor_tensor(v[:, j, :], bank, bv[:, :], ALU.add).then_inc(v_ready, 1)
                elif name[:3] == "OUT":
                    dve.wait_ge(out_mm, R * n + j + 1)
                    dve.wait_ge(bout_added, R * n + R)
                    vec.tensor_tensor(back_h[:, j, :], bank, back_h[:, j, :], ALU.add).then_inc(h2_ready, 1)
                    dve.wait_ge(h2_ready, R * n + j + 1)
                    vec.bn_stats(stats2[:, j, :], back_h[:, j, :]).then_inc(ln2_stats, 1)
                    dve.wait_ge(ln2_stats, 2 * (R * n + j) + 1)
                    wait(dve, ln2_pool, LN2_STEPS * (R * (n - 1) + j + 1))
                    apart(dve, dve_carrier)
                    vec.bn_aggr(mv2[:, j, :], stats2[:, j, :]).then_inc(ln2_stats, 1)

            def ln1(n, t):
                if t == 6:
                    for r in range(R):
                        if r == 0:
                            dve.wait_ge(h_emb_ready, n + 1)
                            dve.wait_ge(conv_ready, n + 1)
                            dve.wait_ge(ext_ready, 2 * n + 2)
                        last = vec.bn_stats(stats1[:, r, :], h_tile(r))
                    chain(n, 5, last)
                    wait(dve, z_ready, R * n)
                    apart(dve, dve_carrier)
                    for r in range(R):
                        last = vec.bn_aggr(mv1[:, r, :], stats1[:, r, :])
                    last.then_inc(ln1_stats, 1)
                if t == 7:
                    dve.wait_ge(ln1_pool, LN1_STEPS * (n + 1))
                    dve.wait_ge(ln1_stats, n + 1)
                    dve.wait_ge(spilled, 64 * (n + 1))
                    for r in range(R):
                        vec.tensor_scalar(h_tile(r), h_tile(r), mv1[:, r, 0:1], rstd1[:, r:r + 1],
                                          ALU.subtract, ALU.mult).then_inc(z_ready, 1)

            def base(n, r):
                dve.wait_ge(xn_ready, R * n + r + 1)
                vec.tensor_scalar(back_h[:, r, :], back_h[:, r, :], coef[:, r, 0:1], coef[:, r, 1:2],
                                  ALU.mult, ALU.add).then_inc(base_ready, 1)

            def route(n, r):
                first = ROUTE_STEPS * (R * n + r)
                done = [0]

                def step(ins):
                    done[0] += 1
                    ins.then_inc(route_vec, 1)
                    dve.wait_ge(route_vec, first + done[0])

                s = sign[:, r % 2, :]
                dve.wait_ge(sign_ready, R * n + r + 1)
                step(vec.tensor_tensor(s, s, slope_sign[:, :], ALU.mult))
                step(vec.reduce_sum(tile_score[:, :], s.rearrange("p (t j) -> p t j", j=DS), X_AXIS))
                step(vec.reduce_sum(cluster_score[:, :], tile_score[:, :].rearrange("p (c t) -> p c t", t=NT // CL), X_AXIS))
                step(vec.scalar_tensor_tensor(cluster_key[:, :], cluster_score[:, :], float(CL), cluster_tie[:, :],
                                              ALU.mult, ALU.add))
                step(vec.scalar_tensor_tensor(tile_key[:, :], tile_score[:, :], float(DS), tile_tie[:, :], ALU.mult, ALU.add))
                step(vec.scalar_tensor_tensor(key[:, :].rearrange("p (c t) -> p c t", t=NT // CL),
                                              cluster_key[:, :].unsqueeze(2).to_broadcast([P, CL, NT // CL]), 256.0,
                                              tile_key[:, :].rearrange("p (c t) -> p c t", t=NT // CL), ALU.mult, ALU.add))
                step(vec.reduce_max(key_max[:, :], key[:, :], X_AXIS))
                wait(dve, masked, R * n + r - 1)
                step(vec.tensor_scalar(onehot[:, r % 2, :], key[:, :], key_max[:, 0:1], None, ALU.is_equal))
                step(vec.tensor_tensor(picked[:, :], onehot[:, r % 2, :], iota_tile[:, :], ALU.mult))
                apart(dve, dve_carrier)
                step(vec.reduce_sum(tile_idx[:, bass.ds(n, 1), r:r + 1], picked[:, :], X_AXIS))
                assert done[0] == CHOOSE_STEPS

            def pick(n, r):
                first = ROUTE_STEPS * (R * n + r) + CHOOSE_STEPS
                done = [0]

                def step(ins):
                    done[0] += 1
                    ins.then_inc(route_vec, 1)
                    dve.wait_ge(route_vec, first + done[0])

                dve.wait_ge(masked, R * n + r + 1)
                oh = onehot[:, r % 2, :]
                apart(dve, dve_carrier)
                step(vec.reduce_sum(slices[:, bass.ds(n, 1), r, :], xf[:, r % 2, :].rearrange("p (t j) -> p j t", j=DS), X_AXIS))
                apart(dve, dve_carrier)
                step(vec.tensor_reduce(tok_ext[:, 0:1], slices[:, bass.ds(n, 1), r, :], X_AXIS, ALU.max))
                apart(dve, dve_carrier)
                step(vec.tensor_reduce(tok_ext[:, 1:2], slices[:, bass.ds(n, 1), r, :], X_AXIS, ALU.min))
                step(vec.tensor_scalar(off_mask[:, :], oh, 1.0, BIG, ALU.subtract, ALU.mult))
                step(vec.scalar_tensor_tensor(cand[:, :], oh, tok_ext[:, 0:1], off_mask[:, :], ALU.mult, ALU.add))
                step(vec.tensor_tensor(tile_max[:, :], tile_max[:, :], cand[:, :], ALU.max))
                step(vec.scalar_tensor_tensor(cand[:, :], oh, tok_ext[:, 1:2], off_mask[:, :], ALU.mult, ALU.subtract))
                step(vec.tensor_tensor(tile_min[:, :], tile_min[:, :], cand[:, :], ALU.min))
                assert done[0] + CHOOSE_STEPS == ROUTE_STEPS

            def batch(b):
                for t in range(SLOTS):
                    g, kt = divmod(t, KT)
                    mn, mg = next_group(b, g)
                    an, ag = group_before(b, g)
                    steps = list(MAX_STEPS[kt]) if present(mn) else []
                    pieces = 4 if kt == 0 and present(an) else 0
                    if t == 1 and present(b + 1):
                        selection_norm(b + 1, 0)
                    if t == 5 and present(b + 1):
                        selection_norm(b + 1, 1)
                    for s in range(max(len(steps), pieces)):
                        if s < len(steps):
                            k = steps[s]
                            dve.wait_ge(max_mm, 64 * mn + 16 * mg + k + 1)
                            if k == 0:
                                wait(dve, shift_ready, 2 * (G * mn + mg))
                            vec.reduce_max(row_max[:, k:k + 1], ps_m[:, k % 2, :], X_AXIS).then_inc(max_ready, 1)
                        if s < pieces:
                            if s == 0:
                                dve.wait_ge(attn_mm, 16 * an + 4 * ag + 4)
                                wait(dve, attn_ready, G * an + ag)
                            cols = slice(s * P, (s + 1) * P)
                            vec.reciprocal(recip[:, cols], ps_s[:, cols]).then_inc(recip_ready, 1)
                    if pieces:
                        dve.wait_ge(recip_ready, 16 * an + 4 * ag + 4)
                        wait(dve, out_mm, R * an)
                        vec.tensor_tensor(attn_t[:, ag, :], ps_v[:, :], recip[:, :], ALU.mult).then_inc(attn_ready, 1)
                    if kt == KT - 1 and present(mn):
                        group = G * mn + mg
                        dve.wait_ge(max_ready, 16 * group + 16)
                        wait(dve, shift_mm, group)
                        vec.tensor_scalar(shift[:, 0:16], row_max[:, :], -1.0, None, ALU.mult).then_inc(shift_ready, 1)
                        dve.wait_ge(shift_ready, 2 * group + 1)
                        vec.scalar_tensor_tensor(shift[:, 16:32], row_max[:, :], -1.0, shift[:, 0:16].bitcast(F32),
                                                 ALU.mult, ALU.subtract).then_inc(shift_ready, 1)
                    for name, offset in UNITS[t]:
                        if present(b + offset):
                            unit(b, name, b + offset)
                    if present(b + 1):
                        ln1(b + 1, t)
                    if present(b - 1):
                        for slot, stage in ((NORM_SLOT, base), (ROUTE_SLOT, route), (PICK_SLOT, pick)):
                            if t in slot:
                                stage(b - 1, slot.index(t))
                    if t == 12 and present(b + 2):
                        embed(b + 2)

            embed(0)
            run_batches(dve, batch)

            chain_end = [0]

            def step(ins):
                ins.then_inc(fin_vec, 1)
                chain_end[0] += 1
                dve.wait_ge(fin_vec, chain_end[0])

            for n in range(B):
                if n >= 2:
                    dve.wait_ge(fin_pe, n)
                vec.tensor_tensor(onehots(n), iota_tile[:, :].unsqueeze(1).to_broadcast([P, R, NT]),
                                  tile_idx[:, n, :].unsqueeze(2).to_broadcast([P, R, NT]), ALU.is_equal).then_inc(fin_vec, 1)
                chain_end[0] += 1
            dve.wait_ge(fin_pe, 1)
            vec.reduce_max(table[:, 258:259], ps_m[0:NT, 0, 0:P], X_AXIS)
            step(vec.tensor_reduce(table[:, 257:258], ps_m[0:NT, 1, 0:P], X_AXIS, ALU.min))
            dve.wait_ge(fin_pe, 2 + B)
            step(vec.tensor_copy(tok[:, :, :], ps_s[:, 0:3 * B * R].rearrange("p (k c) -> p c k", c=3)))
            scale, low, high = (tok[:, c, :] for c in range(3))
            step(vec.tensor_tensor(span[:, :], high, low, ALU.subtract))
            step(vec.tensor_scalar(span[:, :], span[:, :], 1e-8, None, ALU.add))
            step(vec.reciprocal(span[:, :], span[:, :]))
            u = slices[:, :, :, :].rearrange("p b r j -> p (b r) j")
            wide = [P, B * R, DS]
            step(vec.tensor_tensor(u, u, low.unsqueeze(2).to_broadcast(wide), ALU.subtract))
            step(vec.tensor_tensor(u, u, span[:, :].unsqueeze(2).to_broadcast(wide), ALU.mult))
            step(vec.tensor_scalar(u, u, 0.0, float(np.float32(1.0 - 1e-6)), ALU.max, ALU.min))
            step(vec.tensor_scalar(u, u, float(GRID), None, ALU.mult))
            step(vec.tensor_copy(cell_int[:, :, :], u))
            step(vec.tensor_copy(cell[:, :, :], cell_int[:, :, :]))
            step(vec.tensor_tensor(above[:, :, :], cell[:, :, :], u, ALU.is_gt))
            step(vec.tensor_tensor(cell[:, :, :], cell[:, :, :], above[:, :, :], ALU.subtract))
            step(vec.tensor_tensor(u, u, cell[:, :, :], ALU.subtract))
            step(vec.tensor_tensor(place[:, :, :], row_base[:, :, :], tile_idx[:, :, :], ALU.add))
            for n in range(B):
                pair = (ps_t, ps_m)[n % 2]
                dve.wait_ge(fin_pe, 3 + B + n)
                here = u.rearrange("p (b r) j -> p b r j", r=R)[:, n]
                shape = [P, R, DS, GRID]
                tab = pair[:, :, :].rearrange("p a (h s j g) -> p (a h) s j g", h=2, s=2, g=GRID)
                w = work(n)
                cells = cell.rearrange("p (b r) j -> p b r j", r=R)[:, n]
                vec.tensor_tensor(mask(n), cells.unsqueeze(3).to_broadcast(shape),
                                  iota_grid[:, :].unsqueeze(1).unsqueeze(1).to_broadcast(shape), ALU.is_equal)
                vec.tensor_tensor(w, tab[:, :, 1], here.unsqueeze(3).to_broadcast(shape), ALU.mult).then_inc(fin_vec, 1)
                chain_end[0] += 1
                dve.wait_ge(fin_vec, chain_end[0])
                step(vec.tensor_tensor(w, w, tab[:, :, 0], ALU.add))
                step(vec.tensor_tensor(w, w, mask(n), ALU.mult))
                step(vec.reduce_sum(grid_val[:, :, :], w, X_AXIS))
                vec.tensor_tensor(delta[:, n], grid_val[:, :, :], scale[:, n * R:(n + 1) * R].unsqueeze(2).to_broadcast([P, R, DS]),
                                  ALU.mult).then_inc(fin_delta, 1)

        @block.gpsimd
        def _(pool):
            gp = nc.gpsimd

            def gather(n):
                pool.wait_ge(ids_in, 16 * (n + 1))
                if not isinstance(n, int) or n > 0:
                    pool.wait_ge(front_mm, 7 * (n - 1) + 1)
                    pool.wait_ge(sel_exp, 2 * (n - 1) + 1)
                apart(pool, pool_carrier)
                for t in range(KT):
                    gp.indirect_dma_start(out=emb[:, t, :], out_offset=None, in_=io["emb_table"],
                                          in_offset=bass.IndirectOffsetOnAxis(ap=token_ids[:, t:t + 1], axis=0)).then_inc(rows_in, 16)

            def rsqrt(step, dst, src, tmp, width):
                step(gp.tensor_tensor(dst, src, expo[:, 0:width], ALU.pow))
                step(gp.tensor_tensor(tmp, dst, dst, ALU.mult))
                step(gp.tensor_tensor(tmp, tmp, src, ALU.mult))
                apart(pool, pool_carrier)
                step(gp.tensor_scalar(tmp, tmp, -0.5, 1.5, ALU.mult, ALU.add))
                step(gp.tensor_tensor(dst, dst, tmp, ALU.mult))

            def stepper(sem_, first):
                done = [0]

                def step(ins):
                    done[0] += 1
                    ins.then_inc(sem_, 1)
                    pool.wait_ge(sem_, first + done[0])
                return step, done

            def ln1(n):
                pool.wait_ge(ln1_stats, n + 1)
                wait(pool, z_ready, R * n)
                step, done = stepper(ln1_pool, LN1_STEPS * n)
                apart(pool, pool_carrier)
                step(gp.tensor_scalar(scr1[:, 0, :], mv1[:, :, 1], LN_EPS, None, ALU.add))
                rsqrt(step, rstd1[:, :], scr1[:, 0, :], scr1[:, 1, :], R)
                assert done[0] == LN1_STEPS

            def ln2(n, r):
                pool.wait_ge(ln2_stats, 2 * (R * n + r) + 2)
                wait(pool, base_ready, R * (n - 1) + r + 1)
                step, done = stepper(ln2_pool, LN2_STEPS * (R * n + r))
                mean, var = mv2[:, r, 0:1], mv2[:, r, 1:2]
                s, a, tmp, c = (scr2[:, k:k + 1] for k in range(4))
                apart(pool, pool_carrier)
                step(gp.tensor_scalar(s, var, LN_EPS, None, ALU.add))
                rsqrt(step, a, s, tmp, 1)
                step(gp.tensor_tensor(s, var, a, ALU.mult))
                step(gp.tensor_tensor(s, s, a, ALU.mult))
                apart(pool, pool_carrier)
                step(gp.tensor_scalar(s, s, LN_EPS, None, ALU.add))
                rsqrt(step, c, s, tmp, 1)
                step(gp.tensor_tensor(coef[:, r, 2:3], a, c, ALU.mult))
                apart(pool, pool_carrier)
                step(gp.tensor_scalar(coef[:, r, 0:1], a, 1.0, None, ALU.add))
                apart(pool, pool_carrier)
                step(gp.tensor_scalar(tmp, mean, -1.0, None, ALU.mult))
                step(gp.tensor_tensor(coef[:, r, 1:2], tmp, a, ALU.mult))
                step(gp.tensor_tensor(coef[:, r, 3:4], tmp, coef[:, r, 2:3], ALU.mult))
                assert done[0] == LN2_STEPS

            def affine(n, r):
                pool.wait_ge(xn_ready, R * n + r + 1)
                x = xf[:, r % 2, :]
                gp.tensor_tensor(x, x, gamma[:, :], ALU.mult).then_inc(xg_ready, 1)
                pool.wait_ge(xg_ready, R * n + r + 1)
                gp.tensor_tensor(x, x, beta[:, :], ALU.add).then_inc(xf_ready, 1)

            def mask_xf(n, r):
                pool.wait_ge(route_vec, ROUTE_STEPS * (R * n + r) + CHOOSE_STEPS)
                x = xf[:, r % 2, :].rearrange("p (t j) -> p t j", j=DS)
                gp.tensor_tensor(x, x, onehot[:, r % 2, :].unsqueeze(2).to_broadcast([P, NT, DS]), ALU.mult).then_inc(masked, 1)

            def batch(b):
                for t in range(SLOTS):
                    if t in (1, 2, 3) and present(b - 1):
                        for name, _ in UNITS[t]:
                            if name[:3] == "OUT":
                                ln2(b - 1, int(name[3]))
                    if present(b - 1):
                        for slot, stage in ((NORM_SLOT, affine), (PICK_SLOT, mask_xf)):
                            if t in slot:
                                stage(b - 1, slot.index(t))
                    if t == 4 and present(b + 2):
                        gather(b + 2)
                    if t == 6 and present(b + 1):
                        ln1(b + 1)
                    if t == 14 and present(b):
                        pool.wait_ge(back_in, 64 * (b + 1))
                        for r in range(R):
                            gp.tensor_tensor(back_h[:, r, :], back_h[:, r, :], bout[:, :], ALU.add).then_inc(bout_added, 1)

            pool.wait_ge(setup_vec, 2)
            pool.wait_ge(const_in, 16 * CONST_LOADS)
            gather(0)
            run_batches(pool, batch)

            pool.wait_ge(base_out, 64 * B)
            rows8 = io["out"].rearrange("b s (t j) -> (b s t) j", j=DS)
            for n in range(B):
                pool.wait_ge(fin_delta, n + 1)
                for r in range(R):
                    gp.indirect_dma_start(out=rows8, out_offset=bass.IndirectOffsetOnAxis(ap=place[:, n, r:r + 1], axis=0),
                                          in_=delta[:, n, r, :], in_offset=None, compute_op=ALU.add).then_inc(scattered, 16)


def kernel(**inputs):
    import concourse.bacc as bacc
    from concourse.bass_utils import run_bass_kernel_spmd as run

    f32 = np.float32
    arg = {k: np.ascontiguousarray(a) for k, a in inputs.items()}
    half = C // 2
    depths = np.arange(half, dtype=f32)[None, :] / f32(half)
    angles = np.arange(T, dtype=f32)[:, None] * (f32(1.0) / f32(10000.0) ** depths)
    tiles = np.arange(NT)
    data = {
        "x": arg["x"], "emb_table": arg["L0_tok_emb_table"],
        "conv_w": arg["L0_tok_conv_w"].transpose(2, 1, 0), "conv_b": arg["L0_tok_conv_b"],
        "spos0": arg["L0_tok_spos0"], "spos1": arg["L0_tok_spos1"],
        "WqT": arg["L0_attn_Wq"].T, "WkT": arg["L0_attn_Wk"].T, "WvT": arg["L0_attn_Wv"].T, "WoT": arg["L0_attn_Wout"].T,
        "bq": arg["L0_attn_bq"].reshape(G, P).T, "bk": arg["L0_attn_bk"].reshape(G, P).T, "bv": arg["L0_attn_bv"], "bout": arg["L0_attn_bout"],
        "gamma": arg["L0_ffn_ln_gamma"], "beta": arg["L0_ffn_ln_beta"],
        "bases": arg["L0_ffn_spline_bases"], "slopes": arg["L0_ffn_spline_slopes"], "oscale": arg["L0_ffn_output_scale"],
        "posenc": np.concatenate([np.sin(angles), np.cos(angles)], axis=-1).astype(f32),
        "ident": np.eye(P, dtype=f32),
        "iota_tile": tiles.astype(f32), "tile_tie": (NT // CL - 1 - tiles % (NT // CL)).astype(f32),
        "cluster_tie": (CL - 1 - np.arange(CL)).astype(f32), "iota_grid": np.arange(GRID).astype(f32),
        "row_base": (NT * (np.arange(B)[None, :, None] * R * P + np.arange(R)[None, None, :] * P
                           + np.arange(P)[:, None, None])).astype(f32),
    }
    nc = bacc.Bacc("TRN2", target_bir_lowering=False, num_devices=1, dynamic_dma_scratch_size=3072)
    arrays, io = {}, {}
    for name, a in data.items():
        a = np.ascontiguousarray(a)
        arrays[f"in_{name}"] = a
        io[name] = nc.dram_tensor(f"in_{name}", a.shape, mybir.dt.from_np(a.dtype), kind="ExternalInput").ap()
    io["out"] = nc.dram_tensor("out_h", (B, R * P, T), F32, kind="ExternalOutput").ap()
    build(nc, io)
    return run(nc, [arrays], core_ids=[0]).results[0]["out_h"]
```

```python
from contextlib import ExitStack

import numpy as np

import concourse.bass as bass
from concourse import mybir

F32 = mybir.dt.float32
F32R = mybir.dt.float32r
BF16 = mybir.dt.bfloat16
I32 = mybir.dt.int32
ALU = mybir.AluOpType
ACT = mybir.ActivationFunctionType
X_AXIS = mybir.AxisListType.X

P = 128
B = 16
T = 512
C = 128
R = 4
H, DH = 16, 32
G = 4
HG = H // G
KT = T // P
SLOTS = G * KT
NT = 64
DS = 8
CL = 8
GRID = 16
LN_EPS = 1e-5
BIG = 1e30
SCORE_ROWS = 3 * DH
SHIFT_ROWS = SCORE_ROWS + 2

UNITS = [
    [("V3", 0)],
    [("OUT0", -1)],
    [("OUT1", -1)],
    [("MT1", 0), ("OUT2", -1), ("OUT3", -1)],
    [("Q3", 0)],
    [("K3", 0)],
    [("ZT0", 1), ("ZT1", 1), ("ZT2", 1), ("ZT3", 1)],
    [("MT2", 0), ("Q0", 1)],
    [("K0", 1), ("EX", 2)],
    [("Q1", 1)],
    [("SEL0T", 2), ("CONV", 2)],
    [("MT3", 0), ("K1", 1), ("EXT0", 2)],
    [("Q2", 1), ("XCT", 2)],
    [("K2", 1), ("V0", 1)],
    [("V1", 1), ("SEL1T", 2)],
    [("MT0", 1), ("V2", 1), ("EXT1", 2)],
]
ORDER = [u for slot in UNITS for u in slot]
BANK = {name: k % 2 for k, (name, _) in enumerate(ORDER)}
PARTS = {"Q": KT, "K": KT, "V": KT, "O": KT, "C": 3}

MAX_STEPS = [range(0, 4), range(4, 10), range(10, 16), range(16, 16)]

LN2_SLOT = [2, 3, 4, 5]
NORM_SLOT = [4, 6, 8, 10]
SIGN_SLOT = [5, 7, 9, 11]
ROUTE_SLOT = [6, 8, 10, 12]
PICK_SLOT = [7, 9, 11, 13]
RELOAD_SLOT = 12
IDS_SLOT = 0
GATHER_SLOT = 3
EMBED_SLOT = 6
SEL_NORM_SLOT = [10, 14]
STATS_SLOT = [0, 1]
LN1_SLOT = 2
Z_SLOT = [3, 5]
SEL_EXP_SLOT = [9, 13]


def interleave(a, b):
    keyed = [((k + 0.5) / len(x), which, step) for which, x in enumerate((a, b)) for k, step in enumerate(x)]
    return [step for _, _, step in sorted(keyed, key=lambda e: e[:2])]


def order_of_slots():
    slots = []
    for t in range(SLOTS):
        parts = [("U", name, off, p) for name, off in UNITS[t] for p in range(PARTS.get(name[0], 1))]
        rest = interleave([("M", m) for m in MAX_STEPS[t % KT]], parts)
        few = 1 if len(rest) < 8 else 2
        steps = [("S", 0), ("S", 1)] + rest[:2] + [("S", 2)] + rest[2:2 + few] + [("S", 3)] + rest[2 + few:]
        slots.append(steps)
    ordered = []
    for steps in slots:
        outs = {}
        for k, (kind, *unit) in enumerate(steps):
            if kind == "U" and unit[2] == PARTS.get(unit[0][0], 1) - 1:
                at = min(k + 3, len(steps))
                for ahead in range(k + 1, at):
                    if steps[ahead][0] == "U" and BANK[steps[ahead][1]] == BANK[unit[0]]:
                        at = ahead
                        break
                outs.setdefault(at, []).append(("E", unit[0], unit[1]))
        ordered.append([s for k in range(len(steps) + 1) for s in outs.get(k, []) + steps[k:k + 1]])
    return ordered


SLOT_STEPS = order_of_slots()


CONST_LOADS = 20
FRONT_STEPS = 5
LN1_STEPS = 8
LN2_STEPS = 19
CHOOSE_STEPS = 9
ROUTE_STEPS = 17


def run_batches(eng, batch):
    for b in range(-2, 2):
        batch(b)
    with eng.Fori(2, B - 2) as b:
        batch(b)
    for b in range(B - 2, B + 1):
        batch(b)


def present(n):
    return not isinstance(n, int) or 0 <= n < B


def wait(eng, sem, value):
    if isinstance(value, int) and value <= 0:
        return
    eng.wait_ge(sem, value)


def apart(eng, carrier):
    eng.sem_inc(carrier, 1)


def build(nc, io):
    with ExitStack() as ctx:
        def sb(name, shape, dt=F32):
            return ctx.enter_context(nc.sbuf_tensor(name, shape, dt))

        def ps(name, shape):
            return ctx.enter_context(nc.psum_tensor(name, shape, F32))

        def sem(name):
            return ctx.enter_context(nc.semaphore(name))

        q_stack = sb("q_stack", [P, G, HG, T], F32R)
        k_stack = sb("k_stack", [P, G, HG, T], F32R)
        wq = [sb(f"wq_{p}", [P, KT, T], F32R) for p in ("hi", "lo")]
        wk = [sb(f"wk_{p}", [P, KT, T], F32R) for p in ("hi", "lo")]
        wv = [sb(f"wv_{p}", [P, KT, T], F32R) for p in ("hi", "lo")]
        wo = sb("wo", [P, KT, T])
        z_t = [sb(f"z_t_{p}", [P, KT, T], F32R) for p in ("hi", "lo")]
        v = sb("v", [P, KT, T])
        prob = sb("prob", [P, HG, T])
        attn_t = sb("attn_t", [P, KT, T])
        back_h = sb("back_h", [P, R, T])
        h_emb = sb("h_emb", [P, 2 + T])
        h_rest = sb("h_rest", [P, R - 1, T])
        qk_part = [sb(f"qk_{p}", [P, 2, T], F32R) for p in ("hi", "lo")]
        recip = sb("recip", [P, T])
        emb = sb("emb", [P, KT, C])
        sel = sb("sel", [P, KT, C])
        sel_t = sb("sel_t", [P, T])
        posenc = sb("posenc", [P, KT, C])
        xf = sb("xf", [P, 2, T])
        sign = sb("sign", [P, 2, T], BF16)
        gamma = sb("gamma", [P, T])
        beta = sb("beta", [P, T])
        bout = sb("bout", [P, T])
        bv = sb("bv", [P, KT])
        slope_sign = sb("slope_sign", [P, T], BF16)
        conv_w = sb("conv_w", [P, 3, C])
        conv_b = sb("conv_b", [P, 1])
        spos = sb("spos", [P, 2, C])
        ident = sb("ident", [P, P])
        ones = sb("ones", [P, P])
        bqk = sb("bqk", [P, 2, G])
        token_ids = sb("token_ids", [P, KT], I32)
        sel_stat = sb("sel_stat", [P, 4, KT])
        row_max = sb("row_max", [P, HG * KT])
        shift = sb("shift", [P, 2 * HG * KT], F32R)
        shift_t = sb("shift_t", [2 * HG * KT, P], F32R)
        stats1 = sb("stats1", [P, R, 6])
        mv1 = sb("mv1", [P, R, 2])
        rstd1 = sb("rstd1", [P, R])
        shift1 = sb("shift1", [P, R])
        scr1 = sb("scr1", [P, 2, R])
        stats2 = sb("stats2", [P, R, 6])
        mv2 = sb("mv2", [P, R, 2])
        coef = sb("coef", [P, R, 4])
        scr2 = sb("scr2", [P, 8])
        expo = sb("expo", [P, R])
        tile_score = sb("tile_score", [P, NT])
        cluster_score = sb("cluster_score", [P, CL])
        cluster_key = sb("cluster_key", [P, CL])
        tile_key = sb("tile_key", [P, NT])
        key = sb("key", [P, NT])
        key_max = sb("key_max", [P, 1])
        onehot = sb("onehot", [P, 2, NT])
        picked = sb("picked", [P, NT])
        off_mask = sb("off_mask", [P, NT])
        cand = sb("cand", [P, NT])
        tok_ext = sb("tok_ext", [P, 2])
        tile_max = sb("tile_max", [P, NT])
        tile_min = sb("tile_min", [P, NT])
        iota_tile = sb("iota_tile", [P, NT])
        tile_tie = sb("tile_tie", [P, NT])
        cluster_tie = sb("cluster_tie", [P, CL])
        iota_grid = sb("iota_grid", [P, GRID])
        row_base = sb("row_base", [P, B, R])
        tile_idx = sb("tile_idx", [P, B, R])
        slices = sb("slices", [P, B, R, DS])
        table = sb("table", [NT, 2 * DS * GRID + 3])
        mean_slope = sb("mean_slope", [NT, DS])
        tile_sign = sb("tile_sign", [NT, DS])

        def onehots(n):
            return xf[:, n % 2, 0:R * NT].rearrange("p (r t) -> p r t", t=NT)

        def onehot_t4(n):
            return (prob, v, attn_t, back_h)[n // 4][0:NT, n % 4, :]

        def onehot_t(n, r):
            return onehot_t4(n)[:, r * P:(r + 1) * P]

        def by_token(buf):
            return buf.rearrange("p a b -> p (a b)").rearrange("p (k j) -> p k j", j=DS)

        def grids(buf):
            return buf.rearrange("p (r j g) -> p r j g", r=R, j=DS)

        tok = gamma[:, 0:3 * B * R].rearrange("p (c k) -> p c k", c=3)
        span = gamma[:, 3 * B * R:4 * B * R]
        place = beta[:, 0:B * R].bitcast(I32).rearrange("p (b r) -> p b r", r=R)
        grid_val = gamma[:, 4 * B * R:4 * B * R + R * DS].rearrange("p (r j) -> p r j", j=DS)
        cell, above, cell_int = by_token(sel[:, :, :]), by_token(emb[:, :, :]), by_token(posenc[:, :, :].bitcast(I32))
        delta = sel_t[:, :].rearrange("p (b r j) -> p b r j", b=B, r=R)

        def work(n):
            return grids(h_rest[:, n % 2, :])

        def mask(n):
            return grids(recip[:, :] if n % 2 else h_rest[:, 2, :])

        ps_t = ps("ps_t", [P, 2, T])
        ps_m = ps("ps_m", [P, 2, T])
        ps_u = ps("ps_u", [P, 2, T])
        ps_v = ps("ps_v", [P, T])
        ps_s = ps("ps_s", [P, T])

        const_in = sem("const_in")
        weight_in = sem("weight_in")
        weight_hi = sem("weight_hi")
        weight_lo = sem("weight_lo")
        setup_vec = sem("setup_vec")
        sign_row = sem("sign_row")
        sign_bcast = sem("sign_bcast")
        bias_mm = sem("bias_mm")
        ids_in = sem("ids_in")
        rows_in = sem("rows_in")
        emb_ready = sem("emb_ready")
        front_mm = sem("front_mm")
        h_emb_ready = sem("h_emb_ready")
        conv_ready = sem("conv_ready")
        ext_ready = sem("ext_ready")
        sel_max = sem("sel_max")
        sel_exp = sem("sel_exp")
        sel_ready = sem("sel_ready")
        sel_t_ready = sem("sel_t_ready")
        spilled = sem("spilled")
        front_vec = sem("front_vec")
        ln1_stats = sem("ln1_stats")
        ln1_pool = sem("ln1_pool")
        z_ready = sem("z_ready")
        z_mm = sem("z_mm")
        z_hi = sem("z_hi")
        z_lo = sem("z_lo")
        q_mm = sem("q_mm")
        k_mm = sem("k_mm")
        v_mm = sem("v_mm")
        v_ready = sem("v_ready")
        qk_hi_ready = sem("qk_hi_ready")
        qk_lo_ready = sem("qk_lo_ready")
        stack_hi = sem("stack_hi")
        q_stack_in = sem("q_stack_in")
        k_stack_in = sem("k_stack_in")
        max_mm = sem("max_mm")
        max_ready = sem("max_ready")
        shift_ready = sem("shift_ready")
        shift_mm = sem("shift_mm")
        shift_t_ready = sem("shift_t_ready")
        shift_in = sem("shift_in")
        score_mm = sem("score_mm")
        prob_ready = sem("prob_ready")
        attn_mm = sem("attn_mm")
        raw_ready = sem("raw_ready")
        recip_ready = sem("recip_ready")
        attn_ready = sem("attn_ready")
        out_mm = sem("out_mm")
        back_in = sem("back_in")
        bout_added = sem("bout_added")
        h2_ready = sem("h2_ready")
        ln2_stats = sem("ln2_stats")
        ln2_pool = sem("ln2_pool")
        xn_ready = sem("xn_ready")
        xg_ready = sem("xg_ready")
        xf_ready = sem("xf_ready")
        base_ready = sem("base_ready")
        base_out = sem("base_out")
        sign_ready = sem("sign_ready")
        signed_ready = sem("signed_ready")
        route_vec = sem("route_vec")
        masked = sem("masked")
        dve_carrier = sem("dve_carrier")
        pool_carrier = sem("pool_carrier")
        sync_carrier = sem("sync_carrier")
        fin_vec = sem("fin_vec")
        fin_pe = sem("fin_pe")
        fin_act = sem("fin_act")
        fin_delta = sem("fin_delta")
        scattered = sem("scattered")

        freed = {"EX": (h_emb_ready, 1, 1), "SEL0T": (sel_t_ready, 2, 1), "CONV": (conv_ready, 1, 1),
                 "EXT0": (ext_ready, 2, 1), "XCT": (sel_exp, 2, 2), "SEL1T": (sel_t_ready, 2, 2),
                 "EXT1": (ext_ready, 2, 2)}
        for j in range(4):
            freed[f"ZT{j}"] = (z_lo, 4, j + 1)
            freed[f"Q{j}"] = (qk_lo_ready, 8, 2 * j + 1)
            freed[f"K{j}"] = (qk_lo_ready, 8, 2 * j + 2)
            freed[f"V{j}"] = (v_ready, 4, j + 1)
            freed[f"OUT{j}"] = (h2_ready, 4, j + 1)
            freed[f"MT{j}"] = (shift_t_ready, 4, j + 1)

        def wait_bank(pe, b, name):
            at = [u for u, _ in ORDER].index(name)
            for back in range(1, 3 * len(ORDER)):
                k = at - back
                turn, k = k // len(ORDER), k % len(ORDER)
                before, offset = ORDER[k]
                if BANK[before] == BANK[name] and present(b + turn + offset):
                    s, per, within = freed[before]
                    wait(pe, s, (b + turn + offset) * per + within)
                    return

        def unit_bank(name):
            return ps_u[:, BANK[name], :]

        def h_tile(r):
            return h_emb[:, 2:2 + T] if r == 0 else h_rest[:, r - 1, :]

        def next_group(b, g):
            return (b, g + 1) if g < G - 1 else (b + 1, 0)

        def group_before(b, g):
            return (b, g - 1) if g > 0 else (b - 1, G - 1)

        out_rows = io["out"].rearrange("b (r p) t -> b r p t", p=P)
        x_ids = io["x"].rearrange("b (p t) -> b p t", t=KT)

        block = ctx.enter_context(nc.Block())

        @block.sync
        def _(sp):
            weights = [(prob, "WqT"), (v, "WkT"), (attn_t, "WvT"), (wo, "WoT")]
            loads = [(posenc[:, :, :], io["posenc"].rearrange("(p t) c -> p t c", t=KT)),
                     (ident[:, :], io["ident"]),
                     (gamma[:, :], io["gamma"].partition_broadcast(P)), (beta[:, :], io["beta"].partition_broadcast(P)),
                     (bout[:, :], io["bout"].partition_broadcast(P)), (bv[:, :], io["bv"]),
                     (conv_w[:, :, :], io["conv_w"].rearrange("k i o -> i k o")),
                     (conv_b[:, :], io["conv_b"].rearrange("(p o) -> p o", o=1)),
                     (spos[:, 0, :], io["spos0"]), (spos[:, 1, :], io["spos1"]),
                     (bqk[:, 0, :], io["bq"]), (bqk[:, 1, :], io["bk"]),
                     (iota_tile[:, :], io["iota_tile"].partition_broadcast(P)),
                     (tile_tie[:, :], io["tile_tie"].partition_broadcast(P)),
                     (cluster_tie[:, :], io["cluster_tie"].partition_broadcast(P)),
                     (iota_grid[:, :], io["iota_grid"].partition_broadcast(P)),
                     (row_base[:, :, :], io["row_base"]),
                     (table[:, 0:128], io["bases"].rearrange("t j g -> t (j g)")),
                     (table[:, 128:256], io["slopes"].rearrange("t j g -> t (j g)")),
                     (table[:, 256:257], io["oscale"].rearrange("(t o) -> t o", o=1))]
            assert len(loads) == CONST_LOADS
            sp.dma_start(token_ids[:, :], x_ids[0]).then_inc(ids_in, 16)
            for dst, src in loads:
                sp.dma_start(dst, src).then_inc(const_in, 16)
            for dst, name in weights:
                sp.dma_start(dst[:, :, :], io[name].rearrange("(c p) n -> p c n", p=P)).then_inc(weight_in, 16)
            sp.wait_ge(setup_vec, 5)
            sp.dma_start(recip[0:1, :].rearrange("o (t j) -> o t j", j=DS), tile_sign[:, :]).then_inc(sign_row, 16)

            def spill(n, r):
                sp.dma_start(out_rows[n, r], h_tile(r)).then_inc(spilled, 16)

            def to_stack(n, g, which):
                k = n * 8 + 2 * g + which
                stack_in = (q_stack_in, k_stack_in)[which]
                stack = (k_stack if which else q_stack)[:, :, :, :].bitcast(F32)
                hi, lo = (qk_part[p][:, which, :].bitcast(F32) for p in (0, 1))
                again, low = (DH, 2 * DH) if which else (2 * DH, DH)
                sp.wait_ge(qk_hi_ready, k + 1)
                for i in range(HG):
                    sp.dma_start(stack[0:DH, g, i, :], hi[DH * i:DH * (i + 1), :]).then_inc(stack_hi, 16)
                sp.wait_ge(qk_lo_ready, k + 1)
                for i in range(HG):
                    sp.dma_start(stack[low:low + DH, g, i, :], lo[DH * i:DH * (i + 1), :]).then_inc(stack_in, 16)
                sp.wait_ge(stack_hi, 64 * (k + 1))
                apart(sp, sync_carrier)
                sp.dma_start(stack[again:again + DH, g, :, :], stack[0:DH, g, :, :]).then_inc(stack_in, 16)

            def shift_rows(n, g):
                sp.wait_ge(shift_t_ready, n * G + g + 1)
                for part in range(2):
                    row = SCORE_ROWS + part
                    sp.dma_start(q_stack[row:row + 1, g, :, :].bitcast(F32).rearrange("o i (q c) -> o (i q) c", c=P),
                                 shift_t[part * 16:part * 16 + 16, :].bitcast(F32)).then_inc(shift_in, 16)

            def batch(b):
                for t in range(SLOTS):
                    for kind, name, offset in [s for s in SLOT_STEPS[t] if s[0] == "E"]:
                        n = b + offset
                        if not present(n):
                            continue
                        if name == "EX":
                            sp.wait_ge(h_emb_ready, n + 1)
                            spill(n, 0)
                        elif name in ("EXT0", "EXT1"):
                            which = int(name[-1])
                            sp.wait_ge(ext_ready, 2 * n + which + 1)
                            spill(n, 2 * which + 1)
                        elif name == "CONV":
                            sp.wait_ge(conv_ready, n + 1)
                            spill(n, 2)
                        elif name[0] in "QK":
                            to_stack(n, int(name[1]), "QK".index(name[0]))
                        elif name[:2] == "MT":
                            shift_rows(n, int(name[2]))
                    if t in NORM_SLOT and present(b - 1):
                        n, r = b - 1, NORM_SLOT.index(t)
                        sp.wait_ge(base_ready, n * R + r + 1)
                        apart(sp, sync_carrier)
                        sp.dma_start(out_rows[n, r], back_h[:, r, :]).then_inc(base_out, 16)
                    first = isinstance(b, int) and b == -2
                    if t == IDS_SLOT and present(b + 2) and not first:
                        sp.wait_ge(rows_in, 64 * (b + 2))
                        apart(sp, sync_carrier)
                        sp.dma_start(token_ids[:, :], x_ids[b + 2]).then_inc(ids_in, 16)
                    if t == RELOAD_SLOT and present(b):
                        sp.wait_ge(spilled, 64 * (b + 1))
                        apart(sp, sync_carrier)
                        wait(sp, base_out, 64 * b)
                        apart(sp, sync_carrier)
                        for r in range(R):
                            sp.dma_start(back_h[:, r, :], out_rows[b, r]).then_inc(back_in, 16)

            run_batches(sp, batch)
            sp.wait_ge(spilled, 64 * B)
            sp.wait_ge(base_out, 64 * B)
            sp.wait_ge(scattered, 16 * B * R)

        @block.tensor
        def _(pe):
            mm = nc.tensor.matmul

            def transposes(out, ins, n_cols=P):
                for j, a in enumerate(ins):
                    last = nc.tensor.transpose(out[:, j * n_cols:(j + 1) * n_cols], a, ident[:, :])
                return last

            def product3(out, lhs, rhs, c):
                for a, w in ((0, 0), (1, 0), (0, 1)):
                    last = mm(out, lhs(a), rhs(w), start=(c == 0 and a == w), stop=(c == KT - 1 and w == 1))
                return last

            def unit(b, name, n, part):
                bank = unit_bank(name)
                j = int(name[-1]) if name[-1].isdigit() else 0
                if part == 0:
                    if name == "EX":
                        pe.wait_ge(emb_ready, n + 1)
                    elif name in ("SEL0T", "SEL1T"):
                        pe.wait_ge(sel_ready, 2 * n + int(name[3]) + 1)
                    elif name == "CONV":
                        pe.wait_ge(h_emb_ready, n + 1)
                    elif name[:3] == "EXT":
                        pe.wait_ge(sel_t_ready, 2 * n + j + 1)
                    elif name == "XCT":
                        pe.wait_ge(conv_ready, n + 1)
                    elif name[:2] == "ZT":
                        pe.wait_ge(z_ready, R * n + R)
                    elif name[0] in "QKV":
                        pe.wait_ge(z_lo, KT * n + KT)
                    elif name[:3] == "OUT":
                        pe.wait_ge(attn_ready, G * n + G)
                    elif name[:2] == "MT":
                        pe.wait_ge(shift_ready, 2 * (G * n + j) + 2)
                    wait_bank(pe, b, name)
                if name == "EX":
                    transposes(bank, [emb[:, t, :] for t in range(KT)]).then_inc(front_mm, 1)
                elif name in ("SEL0T", "SEL1T"):
                    transposes(bank, [sel[:, t, :] for t in range(KT)]).then_inc(front_mm, 1)
                elif name == "CONV":
                    last = mm(bank, conv_w[:, part, :], h_emb[:, part:part + T], start=(part == 0), stop=(part == 2))
                    if part == 2:
                        last.then_inc(front_mm, 1)
                elif name[:3] == "EXT":
                    mm(bank, spos[:, j, :], sel_t[:, :], start=True, stop=True).then_inc(front_mm, 1)
                elif name == "XCT":
                    transposes(bank, [h_rest[:, 1, t * P:(t + 1) * P] for t in range(KT)]).then_inc(front_mm, 1)
                elif name[:2] == "ZT":
                    transposes(bank, [h_tile(r)[:, j * P:(j + 1) * P] for r in range(R)]).then_inc(z_mm, 1)
                elif name[0] in "QK":
                    w, done = (wq, q_mm) if name[0] == "Q" else (wk, k_mm)
                    last = product3(bank, lambda a: w[a][:, part, j * P:(j + 1) * P], lambda a: z_t[a][:, part, :], part)
                    if part == KT - 1:
                        last.then_inc(done, 1)
                elif name[0] == "V":
                    last = product3(bank, lambda a: z_t[a][:, part, j * P:(j + 1) * P], lambda a: wv[a][:, part, :], part)
                    if part == KT - 1:
                        last.then_inc(v_mm, 1)
                elif name[:3] == "OUT":
                    last = mm(bank, attn_t[:, part, j * P:(j + 1) * P], wo[:, part, :], start=(part == 0), stop=(part == KT - 1))
                    if part == KT - 1:
                        last.then_inc(out_mm, 1)
                elif name[:2] == "MT":
                    nc.tensor.transpose(bank[0:2 * HG * KT, 0:P], shift[:, :].bitcast(F32), ident[:, :]).then_inc(shift_mm, 1)

            def batch(b):
                for t in range(SLOTS):
                    g, kt = divmod(t, KT)
                    mn, mg = next_group(b, g)
                    for step in SLOT_STEPS[t]:
                        if step[0] == "M" and present(mn):
                            s = step[1]
                            i, qt = divmod(s, KT)
                            if s == 0:
                                pe.wait_ge(q_stack_in, 80 * (G * mn + mg + 1))
                                pe.wait_ge(k_stack_in, 80 * (G * mn + mg + 1))
                            wait(pe, max_ready, 64 * mn + 16 * mg + s - 1)
                            mm(ps_m[:, s % 2, :], q_stack[0:SCORE_ROWS, mg, i, qt * P:(qt + 1) * P],
                               k_stack[0:SCORE_ROWS, mg, i, :], start=True, stop=True).then_inc(max_mm, 1)
                        elif step[0] == "S" and present(b):
                            i = step[1]
                            if kt == 0 and i == 0:
                                pe.wait_ge(shift_in, 32 * (G * b + g + 1))
                            wait(pe, prob_ready, 64 * b + 4 * t + i - 1)
                            mm(ps_t[:, i % 2, :], k_stack[0:SHIFT_ROWS, g, i, kt * P:(kt + 1) * P],
                               q_stack[0:SHIFT_ROWS, g, i, :], start=True, stop=True).then_inc(score_mm, 1)
                        elif step[0] == "U" and present(b + step[2]):
                            unit(b, step[1], b + step[2], step[3])
                    if present(b):
                        if g == 0:
                            pe.wait_ge(v_ready, KT * b + kt + 1)
                        if kt == 0:
                            wait(pe, raw_ready, G * b + g)
                        for i in range(HG):
                            hh = HG * g + i
                            pe.wait_ge(prob_ready, 64 * b + 4 * t + i + 1)
                            mm(ps_v[DH * i:DH * (i + 1), :], v[:, kt, DH * hh:DH * (hh + 1)], prob[:, i, :],
                               start=(kt == 0), stop=(kt == KT - 1))
                        for i in range(HG):
                            last = mm(ps_s[DH * i:DH * (i + 1), :], ones[:, 0:DH], prob[:, i, :],
                                      start=(kt == 0), stop=(kt == KT - 1))
                        last.then_inc(attn_mm, 1)

            pe.wait_ge(sign_row, 16)
            pe.wait_ge(setup_vec, 2)
            mm(unit_bank("EX"), ones[0:1, :], recip[0:1, :], start=True, stop=True).then_inc(sign_bcast, 1)
            pe.wait_ge(setup_vec, 6)
            pe.wait_ge(const_in, 16 * CONST_LOADS)
            pe.wait_ge(weight_in, 16 * 4)
            pe.wait_ge(setup_vec, 7)
            for c in range(KT):
                last = mm(unit_bank("EX"), sel[:, c, :], wo[:, c, :], start=(c == 0), stop=(c == KT - 1))
            last.then_inc(bias_mm, 1)
            pe.wait_ge(setup_vec, 8)
            pe.wait_ge(weight_lo, 3)
            run_batches(pe, batch)

            pe.wait_ge(route_vec, ROUTE_STEPS * R * B)
            nc.tensor.transpose(ps_m[0:NT, 0, 0:P], tile_max[:, :], ident[:, :])
            nc.tensor.transpose(ps_m[0:NT, 1, 0:P], tile_min[:, :], ident[:, :]).then_inc(fin_pe, 1)
            for n in range(B):
                pe.wait_ge(fin_vec, 1 + n)
                if n >= 2:
                    pe.wait_ge(fin_act, n - 1)
                for r in range(R):
                    last = nc.tensor.transpose(ps_u[0:NT, n % 2, r * P:(r + 1) * P], onehots(n)[:, r, :], ident[:, :])
                last.then_inc(fin_pe, 1)
            pe.wait_ge(fin_vec, 1 + B)
            for n in range(B):
                pe.wait_ge(fin_act, n + 1)
                for r in range(R):
                    k = 3 * (n * R + r)
                    last = mm(ps_s[:, k:k + 3], onehot_t(n, r), table[:, 256:259], start=True, stop=True)
            last.then_inc(fin_pe, 1)
            for n in range(B):
                pair = (ps_t, ps_m)[n % 2]
                if n >= 2:
                    pe.wait_ge(fin_delta, n - 1)
                for r in range(R):
                    last = mm(pair[:, r // 2, (r % 2) * 256:(r % 2) * 256 + 256], onehot_t(n, r), table[:, 0:256],
                              start=True, stop=True)
                last.then_inc(fin_pe, 1)

        @block.scalar
        def _(act):
            a = nc.scalar.activation
            for k, (src, dst) in enumerate(((prob, wq), (v, wk), (attn_t, wv))):
                act.wait_ge(weight_in, 16 * 4)
                a(dst[0][:, :, :], src[:, :, :], ACT.Copy).then_inc(weight_hi, 1)
            act.wait_ge(const_in, 16 * CONST_LOADS)

            def z_tiles(n, half):
                act.wait_ge(ln1_pool, LN1_STEPS * (n + 1))
                act.wait_ge(spilled, 64 * (n + 1))
                for r in range(2 * half, 2 * half + 2):
                    a(h_tile(r), h_tile(r), ACT.Identity, bias=shift1[:, r:r + 1],
                      scale=rstd1[:, r:r + 1]).then_inc(z_ready, 1)

            def sel_exps(n, which, src):
                act.wait_ge(sel_max, 2 * n + which + 1)
                wait(act, front_mm, 7 * n + (2 if which else -1))
                for t in range(KT):
                    last = a(sel[:, t, :], src[:, t, :], ACT.Exp, bias=sel_stat[:, 1, t:t + 1],
                             accum_out=sel_stat[:, 2, t:t + 1])
                last.then_inc(sel_exp, 1)

            def unit(b, name, n):
                bank = unit_bank(name)
                j = int(name[-1]) if name[-1].isdigit() else 0
                if name == "EX":
                    act.wait_ge(front_mm, 7 * n + 1)
                    wait(act, z_mm, KT * n)
                    a(h_emb[:, 2:2 + T].rearrange("c (p t) -> c t p", t=KT),
                      bank.rearrange("c (t p) -> c t p", t=KT), ACT.Copy).then_inc(h_emb_ready, 1)
                elif name in ("SEL0T", "SEL1T"):
                    j = int(name[3])
                    act.wait_ge(front_mm, 7 * n + (6 if j else 2))
                    wait(act, front_mm, 7 * n + (4 if j else 0))
                    a(sel_t[:, :], bank, ACT.Copy).then_inc(sel_t_ready, 1)
                elif name[:3] == "EXT":
                    act.wait_ge(front_mm, 7 * n + (7 if j else 4))
                    wait(act, z_mm, KT * n)
                    out = h_rest[:, 2 * j, :]
                    if j == 0:
                        out, bank = out.rearrange("c (p t) -> c t p", t=KT), bank.rearrange("c (t p) -> c t p", t=KT)
                    a(out, bank, ACT.Copy).then_inc(ext_ready, 1)
                elif name == "CONV":
                    act.wait_ge(front_mm, 7 * n + 3)
                    wait(act, z_mm, KT * n)
                    a(h_rest[:, 1, :], bank, ACT.Identity, bias=conv_b[:, 0:1]).then_inc(conv_ready, 1)
                elif name[:2] == "ZT":
                    act.wait_ge(z_mm, KT * n + j + 1)
                    wait(act, k_mm, G * n)
                    wait(act, v_mm, KT * n)
                    a(z_t[0][:, j, :], bank, ACT.Copy).then_inc(z_hi, 1)
                elif name[0] in "QK":
                    which = "QK".index(name[0])
                    act.wait_ge((q_mm, k_mm)[which], G * n + j + 1)
                    wait(act, (q_stack_in, k_stack_in)[which], 80 * (G * n + j))
                    a(qk_part[0][:, which, :], bank, ACT.Identity, bias=bqk[:, which, j:j + 1]).then_inc(qk_hi_ready, 1)
                elif name[0] == "V":
                    act.wait_ge(v_mm, KT * n + j + 1)
                    wait(act, attn_mm, 16 * (n - 1) + 12 + j + 1)
                    a(v[:, j, :], bank, ACT.Copy).then_inc(v_ready, 1)
                elif name[:2] == "MT":
                    act.wait_ge(shift_mm, G * n + j + 1)
                    wait(act, shift_in, 32 * (G * n + j))
                    a(shift_t[:, :], bank[0:2 * HG * KT, 0:P], ACT.Copy).then_inc(shift_t_ready, 1)

            def raw(n, g):
                if not present(n):
                    return
                act.wait_ge(attn_mm, 16 * n + 4 * g + 4)
                wait(act, attn_ready, G * n + g)
                a(recip[:, :], ps_s[:, :], ACT.Copy)
                wait(act, out_mm, R * n)
                a(attn_t[:, g, :], ps_v[:, :], ACT.Copy).then_inc(raw_ready, 1)

            def stages(b, t):
                if t in Z_SLOT and present(b + 1):
                    z_tiles(b + 1, Z_SLOT.index(t))
                if t == SEL_EXP_SLOT[0] and present(b + 2):
                    sel_exps(b + 2, 0, emb)
                if t == SEL_EXP_SLOT[1] and present(b + 2):
                    act.wait_ge(front_mm, 7 * (b + 2) + 5)
                    sel_exps(b + 2, 1, unit_bank("XCT").rearrange("p (t c) -> p t c", t=KT))
                n = b - 1
                if present(n) and t in NORM_SLOT:
                    r = NORM_SLOT.index(t)
                    act.wait_ge(ln2_pool, LN2_STEPS * (R * n + r + 1))
                    wait(act, route_vec, ROUTE_STEPS * (R * n + r - 2) + CHOOSE_STEPS + 1)
                    a(xf[:, r % 2, :], back_h[:, r, :], ACT.Identity, bias=coef[:, r, 3:4],
                      scale=coef[:, r, 2:3]).then_inc(xn_ready, 1)
                    act.wait_ge(xn_ready, R * n + r + 1)
                    a(back_h[:, r, :], back_h[:, r, :], ACT.Identity, bias=coef[:, r, 1:2],
                      scale=coef[:, r, 0:1]).then_inc(base_ready, 1)
                if present(n) and t in SIGN_SLOT:
                    r = SIGN_SLOT.index(t)
                    act.wait_ge(xf_ready, R * n + r + 1)
                    wait(act, route_vec, ROUTE_STEPS * (R * n + r - 2) + 1)
                    a(sign[:, r % 2, :], xf[:, r % 2, :], ACT.Sign).then_inc(sign_ready, 1)

            def batch(b):
                for t in range(SLOTS):
                    for step in SLOT_STEPS[t]:
                        if step[0] == "S" and present(b):
                            i = step[1]
                            act.wait_ge(score_mm, 64 * b + 4 * t + i + 1)
                            if i == 0:
                                wait(act, attn_mm, 16 * b + t)
                            a(prob[:, i, :], ps_t[:, i % 2, :], ACT.Exp, scale=float(DH) ** -0.5).then_inc(prob_ready, 1)
                        if step == ("S", 3):
                            stages(b, t)
                        if step == ("S", 1) and t % KT == 0:
                            raw(*group_before(b, t // KT))
                        elif step[0] == "E" and present(b + step[2]):
                            unit(b, step[1], b + step[2])

            run_batches(act, batch)
            act.wait_ge(base_out, 64 * B)
            for n in range(B):
                act.wait_ge(fin_pe, 2 + n)
                a(onehot_t4(n), ps_u[0:NT, n % 2, :], ACT.Copy).then_inc(fin_act, 1)

        @block.vector
        def _(dve):
            vec = nc.vector
            vec.memset(k_stack[SCORE_ROWS:P, :, :, :].bitcast(F32), 1.0).then_inc(setup_vec, 1)
            vec.memset(ones[:, :], 1.0)
            vec.memset(h_emb[:, 0:2], 0.0)
            vec.memset(expo[:, :], -0.5)
            vec.memset(tile_max[:, :], -BIG)
            vec.memset(tile_min[:, :], BIG).then_inc(setup_vec, 1)
            dve.wait_ge(const_in, 16 * CONST_LOADS)
            vec.reduce_sum(mean_slope[:, :], table[:, 128:256].rearrange("t (j g) -> t j g", g=GRID), X_AXIS).then_inc(setup_vec, 1)
            dve.wait_ge(setup_vec, 3)
            vec.tensor_scalar(tile_sign[:, :], mean_slope[:, :], 0.0, None, ALU.is_lt).then_inc(setup_vec, 1)
            dve.wait_ge(setup_vec, 4)
            vec.scalar_tensor_tensor(tile_sign[:, :], mean_slope[:, :], 0.0, tile_sign[:, :],
                                     ALU.is_gt, ALU.subtract).then_inc(setup_vec, 1)
            dve.wait_ge(sign_bcast, 1)
            vec.tensor_copy(slope_sign[:, :], unit_bank("EX")).then_inc(setup_vec, 1)
            for c in range(KT):
                last = vec.tensor_scalar(sel[:, c, :], ones[:, :], bv[:, c:c + 1], None, ALU.mult)
            last.then_inc(setup_vec, 1)
            dve.wait_ge(bias_mm, 1)
            vec.tensor_tensor(bout[:, :], unit_bank("EX"), bout[:, :], ALU.add).then_inc(setup_vec, 1)
            for k, (src, dst) in enumerate(((prob, wq), (v, wk), (attn_t, wv))):
                dve.wait_ge(weight_hi, k + 1)
                vec.tensor_tensor(dst[1][:, :, :], src[:, :, :], dst[0][:, :, :].bitcast(F32), ALU.subtract).then_inc(weight_lo, 1)
            dve.wait_ge(weight_lo, 3)

            def embed(n):
                dve.wait_ge(rows_in, 64 * (n + 1))
                vec.scalar_tensor_tensor(emb[:, :, :], emb[:, :, :], float(np.sqrt(np.float32(C))), posenc[:, :, :],
                                         ALU.mult, ALU.add).then_inc(emb_ready, 1)

            def chain(n, k, ins):
                ins.then_inc(front_vec, 1)
                dve.wait_ge(front_vec, FRONT_STEPS * n + k)

            def selection_max(n, which, src):
                chain(n, 2 * which + 1, vec.reduce_max(sel_stat[:, 0, :], src, X_AXIS))
                ins = vec.tensor_scalar(sel_stat[:, 1, :], sel_stat[:, 0, :], -1.0, None, ALU.mult)
                ins.then_inc(sel_max, 1)

            def selection_norm(n, which):
                dve.wait_ge(sel_exp, 2 * n + which + 1)
                chain(n, 2 * which + 2, vec.reciprocal(sel_stat[:, 3, :], sel_stat[:, 2, :]))
                vec.tensor_tensor(sel[:, :, :], sel[:, :, :], sel_stat[:, 3, :].unsqueeze(2).to_broadcast([P, KT, C]),
                                  ALU.mult).then_inc(sel_ready, 1)

            def unit(b, name, n):
                bank = unit_bank(name)
                j = int(name[-1]) if name[-1].isdigit() else 0
                if name == "EX":
                    dve.wait_ge(emb_ready, n + 1)
                    selection_max(n, 0, emb[:, :, :])
                elif name == "XCT":
                    dve.wait_ge(front_mm, 7 * n + 5)
                    selection_max(n, 1, bank.rearrange("p (t c) -> p t c", t=KT))
                elif name[:2] == "ZT":
                    dve.wait_ge(z_hi, KT * n + j + 1)
                    vec.tensor_tensor(z_t[1][:, j, :], bank, z_t[0][:, j, :].bitcast(F32), ALU.subtract).then_inc(z_lo, 1)
                elif name[0] in "QK":
                    which = "QK".index(name[0])
                    dve.wait_ge(qk_hi_ready, 8 * n + 2 * j + which + 1)
                    vec.scalar_tensor_tensor(qk_part[1][:, which, :], bank, bqk[:, which, j:j + 1],
                                             qk_part[0][:, which, :].bitcast(F32), ALU.add, ALU.subtract).then_inc(qk_lo_ready, 1)
                elif name[:3] == "OUT":
                    dve.wait_ge(out_mm, R * n + j + 1)
                    dve.wait_ge(bout_added, R * n + R)
                    vec.tensor_tensor(back_h[:, j, :], bank, back_h[:, j, :], ALU.add).then_inc(h2_ready, 1)
                    dve.wait_ge(h2_ready, R * n + j + 1)
                    vec.bn_stats(stats2[:, j, :], back_h[:, j, :]).then_inc(ln2_stats, 1)
                    dve.wait_ge(ln2_stats, 2 * (R * n + j) + 1)
                    wait(dve, ln2_pool, LN2_STEPS * (R * (n - 1) + j + 1))
                    apart(dve, dve_carrier)
                    vec.bn_aggr(mv2[:, j, :], stats2[:, j, :]).then_inc(ln2_stats, 1)

            def ln1(n, t):
                if t == STATS_SLOT[0]:
                    dve.wait_ge(h_emb_ready, n + 1)
                    dve.wait_ge(conv_ready, n + 1)
                    dve.wait_ge(ext_ready, 2 * n + 1)
                    for r in range(R - 1):
                        vec.bn_stats(stats1[:, r, :], h_tile(r))
                if t == STATS_SLOT[1]:
                    dve.wait_ge(ext_ready, 2 * n + 2)
                    chain(n, 5, vec.bn_stats(stats1[:, R - 1, :], h_tile(R - 1)))
                    wait(dve, ln1_pool, LN1_STEPS * n)
                    apart(dve, dve_carrier)
                    for r in range(R):
                        last = vec.bn_aggr(mv1[:, r, :], stats1[:, r, :])
                    last.then_inc(ln1_stats, 1)

            def route(n, r):
                first = ROUTE_STEPS * (R * n + r)
                done = [0]

                def step(ins):
                    done[0] += 1
                    ins.then_inc(route_vec, 1)
                    return first + done[0]

                s = sign[:, r % 2, :]
                by_cluster = "p (c t) -> p c t"
                dve.wait_ge(signed_ready, R * n + r + 1)
                yield step(vec.reduce_sum(tile_score[:, :], s.rearrange("p (t j) -> p t j", j=DS), X_AXIS))
                yield step(vec.reduce_sum(cluster_score[:, :], tile_score[:, :].rearrange(by_cluster, t=NT // CL), X_AXIS))
                yield step(vec.scalar_tensor_tensor(cluster_key[:, :], cluster_score[:, :], float(CL), cluster_tie[:, :],
                                                    ALU.mult, ALU.add))
                yield step(vec.scalar_tensor_tensor(tile_key[:, :], tile_score[:, :], float(DS), tile_tie[:, :],
                                                    ALU.mult, ALU.add))
                yield step(vec.scalar_tensor_tensor(key[:, :].rearrange(by_cluster, t=NT // CL),
                                                    cluster_key[:, :].unsqueeze(2).to_broadcast([P, CL, NT // CL]), 256.0,
                                                    tile_key[:, :].rearrange(by_cluster, t=NT // CL), ALU.mult, ALU.add))
                yield step(vec.reduce_max(key_max[:, :], key[:, :], X_AXIS))
                wait(dve, masked, R * n + r - 1)
                yield step(vec.tensor_scalar(onehot[:, r % 2, :], key[:, :], key_max[:, 0:1], None, ALU.is_equal))
                yield step(vec.tensor_tensor(picked[:, :], onehot[:, r % 2, :], iota_tile[:, :], ALU.mult))
                apart(dve, dve_carrier)
                yield step(vec.reduce_sum(tile_idx[:, bass.ds(n, 1), r:r + 1], picked[:, :], X_AXIS))
                assert done[0] == CHOOSE_STEPS

            def pick(n, r):
                first = ROUTE_STEPS * (R * n + r) + CHOOSE_STEPS
                done = [0]

                def step(ins):
                    done[0] += 1
                    ins.then_inc(route_vec, 1)
                    return first + done[0]

                dve.wait_ge(masked, R * n + r + 1)
                oh = onehot[:, r % 2, :]
                apart(dve, dve_carrier)
                yield step(vec.reduce_sum(slices[:, bass.ds(n, 1), r, :], xf[:, r % 2, :].rearrange("p (t j) -> p j t", j=DS), X_AXIS))
                apart(dve, dve_carrier)
                yield step(vec.tensor_reduce(tok_ext[:, 0:1], slices[:, bass.ds(n, 1), r, :], X_AXIS, ALU.max))
                apart(dve, dve_carrier)
                yield step(vec.tensor_reduce(tok_ext[:, 1:2], slices[:, bass.ds(n, 1), r, :], X_AXIS, ALU.min))
                yield step(vec.tensor_scalar(off_mask[:, :], oh, 1.0, BIG, ALU.subtract, ALU.mult))
                yield step(vec.scalar_tensor_tensor(cand[:, :], oh, tok_ext[:, 0:1], off_mask[:, :], ALU.mult, ALU.add))
                yield step(vec.tensor_tensor(tile_max[:, :], tile_max[:, :], cand[:, :], ALU.max))
                yield step(vec.scalar_tensor_tensor(cand[:, :], oh, tok_ext[:, 1:2], off_mask[:, :], ALU.mult, ALU.subtract))
                yield step(vec.tensor_tensor(tile_min[:, :], tile_min[:, :], cand[:, :], ALU.min))
                assert done[0] + CHOOSE_STEPS == ROUTE_STEPS

            def routing(b, t):
                for slot, stage in ((PICK_SLOT, pick), (ROUTE_SLOT, route)):
                    if t in slot and present(b - 1):
                        for count in stage(b - 1, slot.index(t)):
                            yield
                            dve.wait_ge(route_vec, count)

            def batch(b):
                for t in range(SLOTS):
                    g, kt = divmod(t, KT)
                    mn, mg = next_group(b, g)
                    an, ag = group_before(b, g)
                    group = G * mn + mg
                    if t in SEL_NORM_SLOT and present(b + 2):
                        selection_norm(b + 2, SEL_NORM_SLOT.index(t))
                    if kt == KT - 1 and present(mn):
                        dve.wait_ge(max_ready, 16 * group + 16)
                        wait(dve, shift_mm, group)
                        vec.tensor_scalar(shift[:, 0:16], row_max[:, :], -1.0, None, ALU.mult).then_inc(shift_ready, 1)
                        dve.wait_ge(shift_ready, 2 * group + 1)
                        vec.scalar_tensor_tensor(shift[:, 16:32], row_max[:, :], -1.0, shift[:, 0:16].bitcast(F32),
                                                 ALU.mult, ALU.subtract).then_inc(shift_ready, 1)
                    between = routing(b, t)
                    normed = 0 if kt == 0 and present(an) else HG + 1
                    for step in SLOT_STEPS[t]:
                        if step[0] == "M":
                            if present(mn):
                                k = step[1]
                                dve.wait_ge(max_mm, 16 * group + k + 1)
                                if k == 0:
                                    wait(dve, shift_ready, 2 * group)
                                vec.reduce_max(row_max[:, k:k + 1], ps_m[:, k % 2, :], X_AXIS).then_inc(max_ready, 1)
                            if normed < HG:
                                if normed == 0:
                                    dve.wait_ge(raw_ready, G * an + ag + 1)
                                cols = slice(normed * P, (normed + 1) * P)
                                vec.reciprocal(recip[:, cols], recip[:, cols]).then_inc(recip_ready, 1)
                                normed += 1
                                if normed == HG:
                                    dve.wait_ge(recip_ready, 16 * an + 4 * ag + 4)
                                    vec.tensor_tensor(attn_t[:, ag, :], attn_t[:, ag, :], recip[:, :], ALU.mult).then_inc(attn_ready, 1)
                            else:
                                next(between, None)
                        elif step[0] == "E" and present(b + step[2]):
                            unit(b, step[1], b + step[2])
                        elif step[0] == "S" or step[0] == "U":
                            next(between, None)
                    assert normed >= HG
                    for _ in between:
                        pass
                    if present(b + 1):
                        ln1(b + 1, t)
                    if t == EMBED_SLOT and present(b + 2):
                        embed(b + 2)

            run_batches(dve, batch)

            chain_end = [0]

            def step(ins):
                ins.then_inc(fin_vec, 1)
                chain_end[0] += 1
                dve.wait_ge(fin_vec, chain_end[0])

            for n in range(B):
                if n >= 2:
                    dve.wait_ge(fin_pe, n)
                vec.tensor_tensor(onehots(n), iota_tile[:, :].unsqueeze(1).to_broadcast([P, R, NT]),
                                  tile_idx[:, n, :].unsqueeze(2).to_broadcast([P, R, NT]), ALU.is_equal).then_inc(fin_vec, 1)
                chain_end[0] += 1
            dve.wait_ge(fin_pe, 1)
            vec.reduce_max(table[:, 258:259], ps_m[0:NT, 0, 0:P], X_AXIS)
            step(vec.tensor_reduce(table[:, 257:258], ps_m[0:NT, 1, 0:P], X_AXIS, ALU.min))
            dve.wait_ge(fin_pe, 2 + B)
            step(vec.tensor_copy(tok[:, :, :], ps_s[:, 0:3 * B * R].rearrange("p (k c) -> p c k", c=3)))
            scale, low, high = (tok[:, c, :] for c in range(3))
            step(vec.tensor_tensor(span[:, :], high, low, ALU.subtract))
            step(vec.tensor_scalar(span[:, :], span[:, :], 1e-8, None, ALU.add))
            step(vec.reciprocal(span[:, :], span[:, :]))
            u = slices[:, :, :, :].rearrange("p b r j -> p (b r) j")
            wide = [P, B * R, DS]
            step(vec.tensor_tensor(u, u, low.unsqueeze(2).to_broadcast(wide), ALU.subtract))
            step(vec.tensor_tensor(u, u, span[:, :].unsqueeze(2).to_broadcast(wide), ALU.mult))
            step(vec.tensor_scalar(u, u, 0.0, float(np.float32(1.0 - 1e-6)), ALU.max, ALU.min))
            step(vec.tensor_scalar(u, u, float(GRID), None, ALU.mult))
            step(vec.tensor_copy(cell_int[:, :, :], u))
            step(vec.tensor_copy(cell[:, :, :], cell_int[:, :, :]))
            step(vec.tensor_tensor(above[:, :, :], cell[:, :, :], u, ALU.is_gt))
            step(vec.tensor_tensor(cell[:, :, :], cell[:, :, :], above[:, :, :], ALU.subtract))
            step(vec.tensor_tensor(u, u, cell[:, :, :], ALU.subtract))
            step(vec.tensor_tensor(place[:, :, :], row_base[:, :, :], tile_idx[:, :, :], ALU.add))
            for n in range(B):
                pair = (ps_t, ps_m)[n % 2]
                dve.wait_ge(fin_pe, 3 + B + n)
                here = u.rearrange("p (b r) j -> p b r j", r=R)[:, n]
                shape = [P, R, DS, GRID]
                tab = pair[:, :, :].rearrange("p a (h s j g) -> p (a h) s j g", h=2, s=2, g=GRID)
                w = work(n)
                cells = cell.rearrange("p (b r) j -> p b r j", r=R)[:, n]
                vec.tensor_tensor(mask(n), cells.unsqueeze(3).to_broadcast(shape),
                                  iota_grid[:, :].unsqueeze(1).unsqueeze(1).to_broadcast(shape), ALU.is_equal)
                vec.tensor_tensor(w, tab[:, :, 1], here.unsqueeze(3).to_broadcast(shape), ALU.mult).then_inc(fin_vec, 1)
                chain_end[0] += 1
                dve.wait_ge(fin_vec, chain_end[0])
                step(vec.tensor_tensor(w, w, tab[:, :, 0], ALU.add))
                step(vec.tensor_tensor(w, w, mask(n), ALU.mult))
                step(vec.reduce_sum(grid_val[:, :, :], w, X_AXIS))
                vec.tensor_tensor(delta[:, n], grid_val[:, :, :], scale[:, n * R:(n + 1) * R].unsqueeze(2).to_broadcast([P, R, DS]),
                                  ALU.mult).then_inc(fin_delta, 1)

        @block.gpsimd
        def _(pool):
            gp = nc.gpsimd

            def gather(n):
                pool.wait_ge(ids_in, 16 * (n + 1))
                if not isinstance(n, int) or n > 0:
                    pool.wait_ge(front_mm, 7 * (n - 1) + 1)
                    pool.wait_ge(sel_exp, 2 * (n - 1) + 1)
                apart(pool, pool_carrier)
                for t in range(KT):
                    gp.indirect_dma_start(out=emb[:, t, :], out_offset=None, in_=io["emb_table"],
                                          in_offset=bass.IndirectOffsetOnAxis(ap=token_ids[:, t:t + 1], axis=0)).then_inc(rows_in, 16)

            def rsqrt(step, dst, src, tmp, width):
                step(gp.tensor_tensor(dst, src, expo[:, 0:width], ALU.pow))
                step(gp.tensor_tensor(tmp, dst, dst, ALU.mult))
                step(gp.tensor_tensor(tmp, tmp, src, ALU.mult))
                apart(pool, pool_carrier)
                step(gp.tensor_scalar(tmp, tmp, -0.5, 1.5, ALU.mult, ALU.add))
                step(gp.tensor_tensor(dst, dst, tmp, ALU.mult))

            def stepper(sem_, first):
                done = [0]

                def step(ins):
                    done[0] += 1
                    ins.then_inc(sem_, 1)
                    pool.wait_ge(sem_, first + done[0])
                return step, done

            def ln1(n):
                pool.wait_ge(ln1_stats, n + 1)
                wait(pool, z_ready, R * n)
                step, done = stepper(ln1_pool, LN1_STEPS * n)
                apart(pool, pool_carrier)
                step(gp.tensor_scalar(scr1[:, 0, :], mv1[:, :, 1], LN_EPS, None, ALU.add))
                rsqrt(step, rstd1[:, :], scr1[:, 0, :], scr1[:, 1, :], R)
                step(gp.tensor_tensor(shift1[:, :], mv1[:, :, 0], rstd1[:, :], ALU.mult))
                apart(pool, pool_carrier)
                step(gp.tensor_scalar(shift1[:, :], shift1[:, :], -1.0, None, ALU.mult))
                assert done[0] == LN1_STEPS

            def ln2(n, r):
                pool.wait_ge(ln2_stats, 2 * (R * n + r) + 2)
                wait(pool, base_ready, R * (n - 1) + r + 1)
                step, done = stepper(ln2_pool, LN2_STEPS * (R * n + r))
                mean, var = mv2[:, r, 0:1], mv2[:, r, 1:2]
                s, a, tmp, c = (scr2[:, k:k + 1] for k in range(4))
                apart(pool, pool_carrier)
                step(gp.tensor_scalar(s, var, LN_EPS, None, ALU.add))
                rsqrt(step, a, s, tmp, 1)
                step(gp.tensor_tensor(s, var, a, ALU.mult))
                step(gp.tensor_tensor(s, s, a, ALU.mult))
                apart(pool, pool_carrier)
                step(gp.tensor_scalar(s, s, LN_EPS, None, ALU.add))
                rsqrt(step, c, s, tmp, 1)
                step(gp.tensor_tensor(coef[:, r, 2:3], a, c, ALU.mult))
                apart(pool, pool_carrier)
                step(gp.tensor_scalar(coef[:, r, 0:1], a, 1.0, None, ALU.add))
                apart(pool, pool_carrier)
                step(gp.tensor_scalar(tmp, mean, -1.0, None, ALU.mult))
                step(gp.tensor_tensor(coef[:, r, 1:2], tmp, a, ALU.mult))
                step(gp.tensor_tensor(coef[:, r, 3:4], tmp, coef[:, r, 2:3], ALU.mult))
                assert done[0] == LN2_STEPS

            def affine(n, r):
                pool.wait_ge(xn_ready, R * n + r + 1)
                x = xf[:, r % 2, :]
                gp.tensor_tensor(x, x, gamma[:, :], ALU.mult).then_inc(xg_ready, 1)
                pool.wait_ge(xg_ready, R * n + r + 1)
                gp.tensor_tensor(x, x, beta[:, :], ALU.add).then_inc(xf_ready, 1)

            def signed(n, r):
                pool.wait_ge(sign_ready, R * n + r + 1)
                s = sign[:, r % 2, :]
                gp.tensor_tensor(s, s, slope_sign[:, :], ALU.mult).then_inc(signed_ready, 1)

            def mask_xf(n, r):
                pool.wait_ge(route_vec, ROUTE_STEPS * (R * n + r) + CHOOSE_STEPS)
                x = xf[:, r % 2, :].rearrange("p (t j) -> p t j", j=DS)
                gp.tensor_tensor(x, x, onehot[:, r % 2, :].unsqueeze(2).to_broadcast([P, NT, DS]), ALU.mult).then_inc(masked, 1)

            def batch(b):
                for t in range(SLOTS):
                    if t == GATHER_SLOT and present(b + 2):
                        gather(b + 2)
                    if t == LN1_SLOT and present(b + 1):
                        ln1(b + 1)
                    if present(b - 1):
                        for slot, stage in ((ROUTE_SLOT, mask_xf), (SIGN_SLOT, signed), (NORM_SLOT, affine), (LN2_SLOT, ln2)):
                            if t in slot:
                                stage(b - 1, slot.index(t))
                    if t == RELOAD_SLOT + 1 and present(b):
                        pool.wait_ge(back_in, 64 * (b + 1))
                        for r in range(R):
                            gp.tensor_tensor(back_h[:, r, :], back_h[:, r, :], bout[:, :], ALU.add).then_inc(bout_added, 1)

            pool.wait_ge(setup_vec, 8)
            pool.wait_ge(const_in, 16 * CONST_LOADS)
            run_batches(pool, batch)

            pool.wait_ge(base_out, 64 * B)
            rows8 = io["out"].rearrange("b s (t j) -> (b s t) j", j=DS)
            for n in range(B):
                pool.wait_ge(fin_delta, n + 1)
                for r in range(R):
                    gp.indirect_dma_start(out=rows8, out_offset=bass.IndirectOffsetOnAxis(ap=place[:, n, r:r + 1], axis=0),
                                          in_=delta[:, n, r, :], in_offset=None, compute_op=ALU.add).then_inc(scattered, 16)


def kernel(**inputs):
    import concourse.bacc as bacc
    from concourse.bass_utils import run_bass_kernel_spmd as run

    f32 = np.float32
    arg = {k: np.ascontiguousarray(a) for k, a in inputs.items()}
    half = C // 2
    depths = np.arange(half, dtype=f32)[None, :] / f32(half)
    angles = np.arange(T, dtype=f32)[:, None] * (f32(1.0) / f32(10000.0) ** depths)
    tiles = np.arange(NT)
    data = {
        "x": arg["x"], "emb_table": arg["L0_tok_emb_table"],
        "conv_w": arg["L0_tok_conv_w"].transpose(2, 1, 0), "conv_b": arg["L0_tok_conv_b"],
        "spos0": arg["L0_tok_spos0"], "spos1": arg["L0_tok_spos1"],
        "WqT": arg["L0_attn_Wq"].T, "WkT": arg["L0_attn_Wk"].T, "WvT": arg["L0_attn_Wv"].T, "WoT": arg["L0_attn_Wout"].T,
        "bq": arg["L0_attn_bq"].reshape(G, P).T, "bk": arg["L0_attn_bk"].reshape(G, P).T, "bv": arg["L0_attn_bv"].reshape(KT, P).T, "bout": arg["L0_attn_bout"],
        "gamma": arg["L0_ffn_ln_gamma"], "beta": arg["L0_ffn_ln_beta"],
        "bases": arg["L0_ffn_spline_bases"], "slopes": arg["L0_ffn_spline_slopes"], "oscale": arg["L0_ffn_output_scale"],
        "posenc": np.concatenate([np.sin(angles), np.cos(angles)], axis=-1).astype(f32),
        "ident": np.eye(P, dtype=f32),
        "iota_tile": tiles.astype(f32), "tile_tie": (NT // CL - 1 - tiles % (NT // CL)).astype(f32),
        "cluster_tie": (CL - 1 - np.arange(CL)).astype(f32), "iota_grid": np.arange(GRID).astype(f32),
        "row_base": (NT * (np.arange(B)[None, :, None] * R * P + np.arange(R)[None, None, :] * P
                           + np.arange(P)[:, None, None])).astype(f32),
    }
    nc = bacc.Bacc("TRN2", target_bir_lowering=False, num_devices=1, dynamic_dma_scratch_size=3072)
    arrays, io = {}, {}
    for name, a in data.items():
        a = np.ascontiguousarray(a)
        arrays[f"in_{name}"] = a
        io[name] = nc.dram_tensor(f"in_{name}", a.shape, mybir.dt.from_np(a.dtype), kind="ExternalInput").ap()
    io["out"] = nc.dram_tensor("out_h", (B, R * P, T), F32, kind="ExternalOutput").ap()
    build(nc, io)
    return run(nc, [arrays], core_ids=[0]).results[0]["out_h"]
```

```python
from contextlib import ExitStack

import numpy as np

import concourse.bass as bass
from concourse import mybir

F32 = mybir.dt.float32
F32R = mybir.dt.float32r
BF16 = mybir.dt.bfloat16
I32 = mybir.dt.int32
ALU = mybir.AluOpType
ACT = mybir.ActivationFunctionType
X_AXIS = mybir.AxisListType.X

P = 128
B = 16
T = 512
C = 128
R = 4
H, DH = 16, 32
G = 4
HG = H // G
KT = T // P
SLOTS = G * KT
NT = 64
DS = 8
CL = 8
GRID = 16
LN_EPS = 1e-5
BIG = 1e30
SCORE_ROWS = 3 * DH
SHIFT_ROWS = SCORE_ROWS + 2

UNITS = [
    [("V3", 0)],
    [("OUT0", -1)],
    [("OUT1", -1)],
    [("MT1", 0), ("OUT2", -1), ("OUT3", -1)],
    [("Q3", 0)],
    [("K3", 0), ("ZT0", 1)],
    [("ZT1", 1), ("ZT2", 1), ("ZT3", 1)],
    [("MT2", 0), ("Q0", 1)],
    [("K0", 1), ("EX", 2)],
    [("Q1", 1)],
    [("SEL0T", 2), ("CONV", 2)],
    [("MT3", 0), ("K1", 1), ("XCT", 2)],
    [("Q2", 1), ("EXT0", 2)],
    [("K2", 1), ("V0", 1)],
    [("SEL1T", 2), ("V1", 1)],
    [("MT0", 1), ("V2", 1), ("EXT1", 2)],
]
ORDER = [u for slot in UNITS for u in slot]
BANK = {name: k % 2 for k, (name, _) in enumerate(ORDER)}
PARTS = {"Q": KT, "K": KT, "V": KT, "O": KT, "C": 3}

MAX_STEPS = [[(1, s) for s in range(3, 6)], [(1, s) for s in range(6, 11)], [(1, s) for s in range(11, 16)],
             [(2, s) for s in range(0, 3)]]

LN2_SLOT = [2, 4]
NORM_SLOT = [4, 6, 9, 11]
SIGN_SLOT = [5, 7, 10, 12]
ROUTE_SLOT = [7, 9, 11, 14]
PICK_SLOT = [8, 10, 13, 15]
RELOAD_SLOT = 13
IDS_SLOT = 0
GATHER_SLOT = 3
EMBED_SLOT = 5
SEL_NORM_SLOT = [10, 13]
STATS_SLOT = [15, 1]
LN1_SLOT = 2
Z_SLOT = [3, 4]
SEL_EXP_SLOT = [9, 12]


def interleave(a, b):
    keyed = [((k + 0.5) / len(x), which, step) for which, x in enumerate((a, b)) for k, step in enumerate(x)]
    return [step for _, _, step in sorted(keyed, key=lambda e: e[:2])]


def order_of_slots():
    slots = []
    for t in range(SLOTS):
        parts = [("U", name, off, p) for name, off in UNITS[t] for p in range(PARTS.get(name[0], 1))]
        maxima = [("M", *m) for m in MAX_STEPS[t % KT]]
        rest = interleave(maxima[1:], parts)
        few = 1 if len(rest) < 8 else 2
        steps = [("S", 0), maxima[0], ("S", 1)] + rest[:2] + [("S", 2)] + rest[2:2 + few] + [("S", 3)] + rest[2 + few:]
        slots.append((steps, [("PV",), ("SUM",)]))
    ordered = []
    for steps, end in slots:
        outs = {}
        for k, (kind, *unit) in enumerate(steps):
            if kind == "U" and unit[2] == PARTS.get(unit[0][0], 1) - 1:
                at = min(k + 2, len(steps))
                for ahead in range(k + 1, at):
                    if steps[ahead][0] == "U" and BANK[steps[ahead][1]] == BANK[unit[0]]:
                        at = ahead
                        break
                outs.setdefault(at, []).append(("E", unit[0], unit[1]))
        ordered.append([s for k in range(len(steps) + 1) for s in outs.get(k, []) + steps[k:k + 1]] + end)
    return ordered


SLOT_STEPS = order_of_slots()


FRONT_LOADS = 6
CONST_LOADS = 14
AHEAD = 4
FRONT_STEPS = 5
LN1_STEPS = 8
LN2_STEPS = 19
CHOOSE_STEPS = 9
ROUTE_STEPS = 17


def run_batches(eng, batch):
    for b in range(-2, 2):
        batch(b)
    with eng.Fori(2, B - 2) as b:
        batch(b)
    for b in range(B - 2, B + 1):
        batch(b)


def preparing(b, t, slot):
    return isinstance(b, int) and b == -1 and t == slot


def present(n):
    return not isinstance(n, int) or 0 <= n < B


def wait(eng, sem, value):
    if isinstance(value, int) and value <= 0:
        return
    eng.wait_ge(sem, value)


def apart(eng, carrier):
    eng.sem_inc(carrier, 1)


def build(nc, io):
    with ExitStack() as ctx:
        def sb(name, shape, dt=F32):
            return ctx.enter_context(nc.sbuf_tensor(name, shape, dt))

        def ps(name, shape):
            return ctx.enter_context(nc.psum_tensor(name, shape, F32))

        def sem(name):
            return ctx.enter_context(nc.semaphore(name))

        q_stack = sb("q_stack", [P, G, HG, T], F32R)
        k_stack = sb("k_stack", [P, G, HG, T], F32R)
        wq = [sb(f"wq_{p}", [P, KT, T], F32R) for p in ("hi", "lo")]
        wk = [sb(f"wk_{p}", [P, KT, T], F32R) for p in ("hi", "lo")]
        wv = [sb(f"wv_{p}", [P, KT, T], F32R) for p in ("hi", "lo")]
        wo = sb("wo", [P, KT, T])
        z_t = [sb(f"z_t_{p}", [P, KT, T], F32R) for p in ("hi", "lo")]
        v = sb("v", [P, KT, T])
        prob = sb("prob", [P, HG, T])
        attn_t = sb("attn_t", [P, KT, T])
        back_h = sb("back_h", [P, R, T])
        h_emb = sb("h_emb", [P, 2 + T])
        h_rest = sb("h_rest", [P, R - 1, T])
        qk_part = [sb(f"qk_{p}", [P, 2, T], F32R) for p in ("hi", "lo")]
        recip = sb("recip", [P, T])
        emb = sb("emb", [P, KT, C])
        sel = sb("sel", [P, KT, C])
        sel_t = sb("sel_t", [P, T])
        posenc = sb("posenc", [P, KT, C])
        xf = sb("xf", [P, 2, T])
        sign = sb("sign", [P, 2, T], BF16)
        gamma = sb("gamma", [P, T])
        beta = sb("beta", [P, T])
        bout = sb("bout", [P, T])
        bv = sb("bv", [P, KT])
        slope_sign = sb("slope_sign", [P, T], BF16)
        conv_w = sb("conv_w", [P, 3, C])
        conv_b = sb("conv_b", [P, 1])
        spos = sb("spos", [P, 2, C])
        ident = sb("ident", [P, P])
        ones = sb("ones", [P, P])
        bqk = sb("bqk", [P, 2, G])
        token_ids = sb("token_ids", [P, KT], I32)
        sel_stat = sb("sel_stat", [P, 4, KT])
        row_max = sb("row_max", [P, 2, HG * KT])
        shift = sb("shift", [P, 2 * HG * KT], F32R)
        shift_t = sb("shift_t", [2 * HG * KT, P], F32R)
        stats1 = sb("stats1", [P, R, 6])
        mv1 = sb("mv1", [P, R, 2])
        rstd1 = sb("rstd1", [P, R])
        shift1 = sb("shift1", [P, R])
        scr1 = sb("scr1", [P, 2, R])
        stats2 = sb("stats2", [P, R, 6])
        mv2 = sb("mv2", [P, R, 2])
        coef = sb("coef", [P, R, 4])
        scr2 = sb("scr2", [P, 8])
        expo = sb("expo", [P, R])
        tile_score = sb("tile_score", [P, NT])
        cluster_score = sb("cluster_score", [P, CL])
        cluster_key = sb("cluster_key", [P, CL])
        tile_key = sb("tile_key", [P, NT])
        key = sb("key", [P, NT])
        key_max = sb("key_max", [P, 1])
        onehot = sb("onehot", [P, 2, NT])
        picked = sb("picked", [P, NT])
        off_mask = sb("off_mask", [P, NT])
        cand = sb("cand", [P, NT])
        tok_ext = sb("tok_ext", [P, 2])
        tile_max = sb("tile_max", [P, NT])
        tile_min = sb("tile_min", [P, NT])
        iota_tile = sb("iota_tile", [P, NT])
        tile_tie = sb("tile_tie", [P, NT])
        cluster_tie = sb("cluster_tie", [P, CL])
        iota_grid = sb("iota_grid", [P, GRID])
        row_base = sb("row_base", [P, B, R])
        tile_idx = sb("tile_idx", [P, B, R])
        slices = sb("slices", [P, B, R, DS])
        table = sb("table", [NT, 2 * DS * GRID + 3])
        mean_slope = sb("mean_slope", [NT, DS])
        tile_sign = sb("tile_sign", [NT, DS])

        def onehots(n):
            return xf[:, n % 2, 0:R * NT].rearrange("p (r t) -> p r t", t=NT)

        def onehot_t4(n):
            return (prob, v, attn_t, back_h)[n // 4][0:NT, n % 4, :]

        def onehot_t(n, r):
            return onehot_t4(n)[:, r * P:(r + 1) * P]

        def by_token(buf):
            return buf.rearrange("p a b -> p (a b)").rearrange("p (k j) -> p k j", j=DS)

        def grids(buf):
            return buf.rearrange("p (r j g) -> p r j g", r=R, j=DS)

        tok = gamma[:, 0:3 * B * R].rearrange("p (c k) -> p c k", c=3)
        span = gamma[:, 3 * B * R:4 * B * R]
        place = beta[:, 0:B * R].bitcast(I32).rearrange("p (b r) -> p b r", r=R)
        grid_val = gamma[:, 4 * B * R:4 * B * R + R * DS].rearrange("p (r j) -> p r j", j=DS)
        cell, above, cell_int = by_token(sel[:, :, :]), by_token(emb[:, :, :]), by_token(posenc[:, :, :].bitcast(I32))
        delta = sel_t[:, :].rearrange("p (b r j) -> p b r j", b=B, r=R)

        def work(n):
            return grids(h_rest[:, n % 2, :])

        def mask(n):
            return grids(recip[:, :] if n % 2 else h_rest[:, 2, :])

        ps_t = ps("ps_t", [P, 2, T])
        ps_m = ps("ps_m", [P, 2, T])
        ps_u = ps("ps_u", [P, 2, T])
        ps_v = ps("ps_v", [P, T])
        ps_s = ps("ps_s", [P, T])

        front_in = sem("front_in")
        const_in = sem("const_in")
        weight_in = sem("weight_in")
        weight_hi = sem("weight_hi")
        weight_lo = sem("weight_lo")
        setup_vec = sem("setup_vec")
        sign_row = sem("sign_row")
        sign_bcast = sem("sign_bcast")
        bias_mm = sem("bias_mm")
        ids_in = sem("ids_in")
        rows_in = sem("rows_in")
        emb_ready = sem("emb_ready")
        front_mm = sem("front_mm")
        h_emb_ready = sem("h_emb_ready")
        conv_ready = sem("conv_ready")
        ext_ready = sem("ext_ready")
        sel_max = sem("sel_max")
        sel_exp = sem("sel_exp")
        sel_ready = sem("sel_ready")
        sel_t_ready = sem("sel_t_ready")
        spilled = sem("spilled")
        front_vec = sem("front_vec")
        ln1_stats = sem("ln1_stats")
        ln1_pool = sem("ln1_pool")
        z_ready = sem("z_ready")
        z_mm = sem("z_mm")
        z_hi = sem("z_hi")
        z_lo = sem("z_lo")
        q_mm = sem("q_mm")
        k_mm = sem("k_mm")
        v_mm = sem("v_mm")
        v_ready = sem("v_ready")
        qk_hi_ready = sem("qk_hi_ready")
        qk_lo_ready = sem("qk_lo_ready")
        stack_hi = sem("stack_hi")
        q_stack_in = sem("q_stack_in")
        k_stack_in = sem("k_stack_in")
        max_mm = sem("max_mm")
        max_ready = sem("max_ready")
        shift_ready = sem("shift_ready")
        shift_mm = sem("shift_mm")
        shift_t_ready = sem("shift_t_ready")
        shift_in = sem("shift_in")
        score_mm = sem("score_mm")
        prob_ready = sem("prob_ready")
        attn_mm = sem("attn_mm")
        raw_ready = sem("raw_ready")
        recip_ready = sem("recip_ready")
        attn_ready = sem("attn_ready")
        out_mm = sem("out_mm")
        back_in = sem("back_in")
        bout_added = sem("bout_added")
        h2_ready = sem("h2_ready")
        ln2_stats = sem("ln2_stats")
        ln2_pool = sem("ln2_pool")
        xn_ready = sem("xn_ready")
        xg_ready = sem("xg_ready")
        xf_ready = sem("xf_ready")
        base_ready = sem("base_ready")
        base_out = sem("base_out")
        sign_ready = sem("sign_ready")
        signed_ready = sem("signed_ready")
        route_vec = sem("route_vec")
        masked = sem("masked")
        dve_carrier = sem("dve_carrier")
        pool_carrier = sem("pool_carrier")
        sync_carrier = sem("sync_carrier")
        fin_vec = sem("fin_vec")
        fin_pe = sem("fin_pe")
        fin_tok = sem("fin_tok")
        fin_tab = sem("fin_tab")
        fin_act = sem("fin_act")
        fin_delta = sem("fin_delta")
        fin_free = sem("fin_free")
        scattered = sem("scattered")

        freed = {"EX": (h_emb_ready, 1, 1), "SEL0T": (sel_t_ready, 2, 1), "CONV": (conv_ready, 1, 1),
                 "EXT0": (ext_ready, 2, 1), "XCT": (sel_exp, 2, 2), "SEL1T": (sel_t_ready, 2, 2),
                 "EXT1": (ext_ready, 2, 2)}
        for j in range(4):
            freed[f"ZT{j}"] = (z_lo, 4, j + 1)
            freed[f"Q{j}"] = (qk_lo_ready, 8, 2 * j + 1)
            freed[f"K{j}"] = (qk_lo_ready, 8, 2 * j + 2)
            freed[f"V{j}"] = (v_ready, 4, j + 1)
            freed[f"OUT{j}"] = (h2_ready, 4, j + 1)
            freed[f"MT{j}"] = (shift_t_ready, 4, j + 1)

        def wait_bank(pe, b, name):
            at = [u for u, _ in ORDER].index(name)
            for back in range(1, 3 * len(ORDER)):
                k = at - back
                turn, k = k // len(ORDER), k % len(ORDER)
                before, offset = ORDER[k]
                if BANK[before] == BANK[name] and present(b + turn + offset):
                    s, per, within = freed[before]
                    wait(pe, s, (b + turn + offset) * per + within)
                    return

        def unit_bank(name):
            return ps_u[:, BANK[name], :]

        def h_tile(r):
            return h_emb[:, 2:2 + T] if r == 0 else h_rest[:, r - 1, :]

        def next_group(b, g, ahead=1):
            return (b, g + ahead) if g + ahead < G else (b + 1, g + ahead - G)

        def group_before(b, g):
            return (b, g - 1) if g > 0 else (b - 1, G - 1)

        out_rows = io["out"].rearrange("b (r p) t -> b r p t", p=P)
        x_ids = io["x"].rearrange("b (p t) -> b p t", t=KT)

        block = ctx.enter_context(nc.Block())

        @block.sync
        def _(sp):
            weights = [(prob, "WqT"), (v, "WkT"), (attn_t, "WvT"), (wo, "WoT")]
            front_loads = [(posenc[:, :, :], io["posenc"].rearrange("(p t) c -> p t c", t=KT)),
                           (ident[:, :], io["ident"]),
                           (conv_w[:, :, :], io["conv_w"].rearrange("k i o -> i k o")),
                           (conv_b[:, :], io["conv_b"].rearrange("(p o) -> p o", o=1)),
                           (spos[:, 0, :], io["spos0"]), (spos[:, 1, :], io["spos1"])]
            loads = [(gamma[:, :], io["gamma"].partition_broadcast(P)), (beta[:, :], io["beta"].partition_broadcast(P)),
                     (bout[:, :], io["bout"].partition_broadcast(P)), (bv[:, :], io["bv"]),
                     (bqk[:, 0, :], io["bq"]), (bqk[:, 1, :], io["bk"]),
                     (iota_tile[:, :], io["iota_tile"].partition_broadcast(P)),
                     (tile_tie[:, :], io["tile_tie"].partition_broadcast(P)),
                     (cluster_tie[:, :], io["cluster_tie"].partition_broadcast(P)),
                     (iota_grid[:, :], io["iota_grid"].partition_broadcast(P)),
                     (row_base[:, :, :], io["row_base"]),
                     (table[:, 0:128], io["bases"].rearrange("t j g -> t (j g)")),
                     (table[:, 128:256], io["slopes"].rearrange("t j g -> t (j g)")),
                     (table[:, 256:257], io["oscale"].rearrange("(t o) -> t o", o=1))]
            assert len(loads) == CONST_LOADS
            sp.dma_start(token_ids[:, :], x_ids[0]).then_inc(ids_in, 16)
            assert len(front_loads) == FRONT_LOADS
            for dst, src in front_loads:
                sp.dma_start(dst, src).then_inc(front_in, 16)
            sp.wait_ge(rows_in, 64)
            for dst, name in weights:
                sp.dma_start(dst[:, :, :], io[name].rearrange("(c p) n -> p c n", p=P)).then_inc(weight_in, 16)
            for dst, src in loads:
                sp.dma_start(dst, src).then_inc(const_in, 16)
            def prepare():
                sp.wait_ge(setup_vec, 5)
                sp.dma_start(recip[0:1, :].rearrange("o (t j) -> o t j", j=DS), tile_sign[:, :]).then_inc(sign_row, 16)

            def spill(n, r):
                sp.dma_start(out_rows[n, r], h_tile(r)).then_inc(spilled, 16)

            def to_stack(n, g, which):
                k = n * 8 + 2 * g + which
                stack_in = (q_stack_in, k_stack_in)[which]
                stack = (k_stack if which else q_stack)[:, :, :, :].bitcast(F32)
                hi, lo = (qk_part[p][:, which, :].bitcast(F32) for p in (0, 1))
                again, low = (DH, 2 * DH) if which else (2 * DH, DH)
                sp.wait_ge(qk_hi_ready, k + 1)
                for i in range(HG):
                    sp.dma_start(stack[0:DH, g, i, :], hi[DH * i:DH * (i + 1), :]).then_inc(stack_hi, 16)
                sp.wait_ge(qk_lo_ready, k + 1)
                for i in range(HG):
                    sp.dma_start(stack[low:low + DH, g, i, :], lo[DH * i:DH * (i + 1), :]).then_inc(stack_in, 16)
                sp.wait_ge(stack_hi, 64 * (k + 1))
                apart(sp, sync_carrier)
                sp.dma_start(stack[again:again + DH, g, :, :], stack[0:DH, g, :, :]).then_inc(stack_in, 16)

            def shift_rows(n, g):
                sp.wait_ge(shift_t_ready, n * G + g + 1)
                for part in range(2):
                    row = SCORE_ROWS + part
                    sp.dma_start(q_stack[row:row + 1, g, :, :].bitcast(F32).rearrange("o i (q c) -> o (i q) c", c=P),
                                 shift_t[part * 16:part * 16 + 16, :].bitcast(F32)).then_inc(shift_in, 16)

            def batch(b):
                for t in range(SLOTS):
                    if preparing(b, t, 0):
                        prepare()
                    for kind, name, offset in [s for s in SLOT_STEPS[t] if s[0] == "E"]:
                        n = b + offset
                        if not present(n):
                            continue
                        if name == "EX":
                            sp.wait_ge(h_emb_ready, n + 1)
                            spill(n, 0)
                        elif name in ("EXT0", "EXT1"):
                            which = int(name[-1])
                            sp.wait_ge(ext_ready, 2 * n + which + 1)
                            spill(n, 2 * which + 1)
                        elif name == "CONV":
                            sp.wait_ge(conv_ready, n + 1)
                            spill(n, 2)
                        elif name[0] in "QK":
                            to_stack(n, int(name[1]), "QK".index(name[0]))
                        elif name[:2] == "MT":
                            shift_rows(n, int(name[2]))
                    if t in NORM_SLOT and present(b - 1):
                        n, r = b - 1, NORM_SLOT.index(t)
                        sp.wait_ge(base_ready, n * R + r + 1)
                        apart(sp, sync_carrier)
                        sp.dma_start(out_rows[n, r], back_h[:, r, :]).then_inc(base_out, 16)
                    first = isinstance(b, int) and b == -2
                    if t == IDS_SLOT and present(b + 2) and not first:
                        sp.wait_ge(rows_in, 64 * (b + 2))
                        apart(sp, sync_carrier)
                        sp.dma_start(token_ids[:, :], x_ids[b + 2]).then_inc(ids_in, 16)
                    if t == RELOAD_SLOT and present(b):
                        sp.wait_ge(spilled, 64 * (b + 1))
                        apart(sp, sync_carrier)
                        wait(sp, base_out, 64 * b)
                        apart(sp, sync_carrier)
                        for r in range(R):
                            sp.dma_start(back_h[:, r, :], out_rows[b, r]).then_inc(back_in, 16)

            run_batches(sp, batch)
            sp.wait_ge(spilled, 64 * B)
            sp.wait_ge(base_out, 64 * B)
            sp.wait_ge(scattered, 16 * B * R)

        @block.tensor
        def _(pe):
            mm = nc.tensor.matmul

            def transposes(out, ins, n_cols=P):
                for j, a in enumerate(ins):
                    last = nc.tensor.transpose(out[:, j * n_cols:(j + 1) * n_cols], a, ident[:, :])
                return last

            def product3(out, lhs, rhs, c):
                for a, w in ((0, 0), (1, 0), (0, 1)):
                    last = mm(out, lhs(a), rhs(w), start=(c == 0 and a == w), stop=(c == KT - 1 and w == 1))
                return last

            def unit(b, name, n, part):
                bank = unit_bank(name)
                j = int(name[-1]) if name[-1].isdigit() else 0
                if part == 0:
                    if name == "EX":
                        pe.wait_ge(emb_ready, n + 1)
                    elif name in ("SEL0T", "SEL1T"):
                        pe.wait_ge(sel_ready, 2 * n + int(name[3]) + 1)
                    elif name == "CONV":
                        pe.wait_ge(h_emb_ready, n + 1)
                    elif name[:3] == "EXT":
                        pe.wait_ge(sel_t_ready, 2 * n + j + 1)
                    elif name == "XCT":
                        pe.wait_ge(conv_ready, n + 1)
                    elif name[:2] == "ZT":
                        pe.wait_ge(z_ready, R * n + R)
                    elif name[0] in "QKV":
                        pe.wait_ge(z_lo, KT * n + KT)
                    elif name[:3] == "OUT":
                        pe.wait_ge(attn_ready, G * n + G)
                    elif name[:2] == "MT":
                        pe.wait_ge(shift_ready, 2 * (G * n + j) + 2)
                    wait_bank(pe, b, name)
                if name == "EX":
                    transposes(bank, [emb[:, t, :] for t in range(KT)]).then_inc(front_mm, 1)
                elif name in ("SEL0T", "SEL1T"):
                    transposes(bank, [sel[:, t, :] for t in range(KT)]).then_inc(front_mm, 1)
                elif name == "CONV":
                    last = mm(bank, conv_w[:, part, :], h_emb[:, part:part + T], start=(part == 0), stop=(part == 2))
                    if part == 2:
                        last.then_inc(front_mm, 1)
                elif name[:3] == "EXT":
                    mm(bank, spos[:, j, :], sel_t[:, :], start=True, stop=True).then_inc(front_mm, 1)
                elif name == "XCT":
                    transposes(bank, [h_rest[:, 1, t * P:(t + 1) * P] for t in range(KT)]).then_inc(front_mm, 1)
                elif name[:2] == "ZT":
                    transposes(bank, [h_tile(r)[:, j * P:(j + 1) * P] for r in range(R)]).then_inc(z_mm, 1)
                elif name[0] in "QK":
                    w, done = (wq, q_mm) if name[0] == "Q" else (wk, k_mm)
                    last = product3(bank, lambda a: w[a][:, part, j * P:(j + 1) * P], lambda a: z_t[a][:, part, :], part)
                    if part == KT - 1:
                        last.then_inc(done, 1)
                elif name[0] == "V":
                    last = product3(bank, lambda a: z_t[a][:, part, j * P:(j + 1) * P], lambda a: wv[a][:, part, :], part)
                    if part == KT - 1:
                        last.then_inc(v_mm, 1)
                elif name[:3] == "OUT":
                    last = mm(bank, attn_t[:, part, j * P:(j + 1) * P], wo[:, part, :], start=(part == 0), stop=(part == KT - 1))
                    if part == KT - 1:
                        last.then_inc(out_mm, 1)
                elif name[:2] == "MT":
                    nc.tensor.transpose(bank[0:2 * HG * KT, 0:P], shift[:, :].bitcast(F32), ident[:, :]).then_inc(shift_mm, 1)

            def batch(b):
                for t in range(SLOTS):
                    g, kt = divmod(t, KT)
                    if preparing(b, t, 5):
                        prepare()
                    for step in SLOT_STEPS[t]:
                        mn, mg = next_group(b, g, step[1]) if step[0] == "M" else (B, 0)
                        if present(mn):
                            s = step[2]
                            i, qt = divmod(s, KT)
                            if s == 0:
                                pe.wait_ge(q_stack_in, 80 * (G * mn + mg + 1))
                                pe.wait_ge(k_stack_in, 80 * (G * mn + mg + 1))
                            wait(pe, max_ready, 64 * mn + 16 * mg + s - 1)
                            mm(ps_m[:, s % 2, :], q_stack[0:SCORE_ROWS, mg, i, qt * P:(qt + 1) * P],
                               k_stack[0:SCORE_ROWS, mg, i, :], start=True, stop=True).then_inc(max_mm, 1)
                        elif step[0] == "S" and present(b):
                            i = step[1]
                            if kt == 0 and i == 0:
                                pe.wait_ge(shift_in, 32 * (G * b + g + 1))
                            wait(pe, prob_ready, 64 * b + 4 * t + i - 1)
                            mm(ps_t[:, i % 2, :], k_stack[0:SHIFT_ROWS, g, i, kt * P:(kt + 1) * P],
                               q_stack[0:SHIFT_ROWS, g, i, :], start=True, stop=True).then_inc(score_mm, 1)
                        elif step[0] == "U" and present(b + step[2]):
                            unit(b, step[1], b + step[2], step[3])
                        elif step[0] == "PV" and present(b):
                            if g == 0:
                                pe.wait_ge(v_ready, KT * b + kt + 1)
                            if kt == 0:
                                wait(pe, raw_ready, G * b + g)
                            for i in range(HG):
                                hh = HG * g + i
                                pe.wait_ge(prob_ready, 64 * b + 4 * t + i + 1)
                                mm(ps_v[DH * i:DH * (i + 1), :], v[:, kt, DH * hh:DH * (hh + 1)], prob[:, i, :],
                                   start=(kt == 0), stop=(kt == KT - 1))
                        elif step[0] == "SUM" and present(b):
                            for i in range(HG):
                                last = mm(ps_s[DH * i:DH * (i + 1), :], ones[:, 0:DH], prob[:, i, :],
                                          start=(kt == 0), stop=(kt == KT - 1))
                            last.then_inc(attn_mm, 1)

            def prepare():
                pe.wait_ge(sign_row, 16)
                pe.wait_ge(setup_vec, 2)
                mm(unit_bank("EX"), ones[0:1, :], recip[0:1, :], start=True, stop=True).then_inc(sign_bcast, 1)
                pe.wait_ge(setup_vec, 6)
                pe.wait_ge(weight_in, 16 * 4)
                pe.wait_ge(setup_vec, 7)
                for c in range(KT):
                    last = mm(unit_bank("EX"), sel[:, c, :], wo[:, c, :], start=(c == 0), stop=(c == KT - 1))
                last.then_inc(bias_mm, 1)
                pe.wait_ge(setup_vec, 8)
                pe.wait_ge(weight_lo, 3)

            pe.wait_ge(setup_vec, 2)
            pe.wait_ge(front_in, 16 * FRONT_LOADS)
            run_batches(pe, batch)

            pe.wait_ge(route_vec, ROUTE_STEPS * R * B)
            nc.tensor.transpose(ps_m[0:NT, 0, 0:P], tile_max[:, :], ident[:, :])
            nc.tensor.transpose(ps_m[0:NT, 1, 0:P], tile_min[:, :], ident[:, :]).then_inc(fin_pe, 1)
            for n in range(B):
                pe.wait_ge(fin_vec, 1 + n)
                if n >= 2:
                    pe.wait_ge(fin_act, n - 1)
                for r in range(R):
                    last = nc.tensor.transpose(ps_u[0:NT, n % 2, r * P:(r + 1) * P], onehots(n)[:, r, :], ident[:, :])
                last.then_inc(fin_pe, 1)
            pe.wait_ge(fin_vec, 1 + B)

            def rows_of(n):
                pe.wait_ge(fin_act, n + 1)
                for r in range(R):
                    k = 3 * (n * R + r)
                    bank = (ps_s, ps_v)[n // AHEAD % 2]
                    last = mm(bank[:, k:k + 3], onehot_t(n, r), table[:, 256:259], start=True, stop=True)
                return last

            for n in range(AHEAD):
                last = rows_of(n)
            last.then_inc(fin_tok, 1)
            for n in range(B):
                pair = (ps_t, ps_m)[n % 2]
                if n >= 2:
                    pe.wait_ge(fin_free, n - 1)
                for r in range(R):
                    last = mm(pair[:, r // 2, (r % 2) * 256:(r % 2) * 256 + 256], onehot_t(n, r), table[:, 0:256],
                              start=True, stop=True)
                last.then_inc(fin_tab, 1)
                if n + AHEAD < B:
                    last = rows_of(n + AHEAD)
                    if n % AHEAD == AHEAD - 1:
                        last.then_inc(fin_tok, 1)

        @block.scalar
        def _(act):
            a = nc.scalar.activation
            def prepare():
                act.wait_ge(weight_in, 16 * 4)
                for src, dst in ((prob, wq), (v, wk), (attn_t, wv)):
                    a(dst[0][:, :, :], src[:, :, :], ACT.Copy).then_inc(weight_hi, 1)
                act.wait_ge(const_in, 16 * CONST_LOADS)


            def z_tiles(n, half):
                act.wait_ge(ln1_pool, LN1_STEPS * (n + 1))
                act.wait_ge(spilled, 64 * (n + 1))
                for r in range(2 * half, 2 * half + 2):
                    a(h_tile(r), h_tile(r), ACT.Identity, bias=shift1[:, r:r + 1],
                      scale=rstd1[:, r:r + 1]).then_inc(z_ready, 1)

            def sel_exps(n, which, src):
                act.wait_ge(sel_max, 2 * n + which + 1)
                wait(act, front_mm, 7 * n + (2 if which else -1))
                for t in range(KT):
                    last = a(sel[:, t, :], src[:, t, :], ACT.Exp, bias=sel_stat[:, 1, t:t + 1],
                             accum_out=sel_stat[:, 2, t:t + 1])
                last.then_inc(sel_exp, 1)

            def unit(b, name, n):
                bank = unit_bank(name)
                j = int(name[-1]) if name[-1].isdigit() else 0
                if name == "EX":
                    act.wait_ge(front_mm, 7 * n + 1)
                    wait(act, z_mm, KT * n)
                    a(h_emb[:, 2:2 + T].rearrange("c (p t) -> c t p", t=KT),
                      bank.rearrange("c (t p) -> c t p", t=KT), ACT.Copy).then_inc(h_emb_ready, 1)
                elif name in ("SEL0T", "SEL1T"):
                    j = int(name[3])
                    act.wait_ge(front_mm, 7 * n + (6 if j else 2))
                    wait(act, front_mm, 7 * n + (5 if j else 0))
                    a(sel_t[:, :], bank, ACT.Copy).then_inc(sel_t_ready, 1)
                elif name[:3] == "EXT":
                    act.wait_ge(front_mm, 7 * n + (7 if j else 5))
                    wait(act, z_mm, KT * n)
                    out = h_rest[:, 2 * j, :]
                    if j == 0:
                        out, bank = out.rearrange("c (p t) -> c t p", t=KT), bank.rearrange("c (t p) -> c t p", t=KT)
                    a(out, bank, ACT.Copy).then_inc(ext_ready, 1)
                elif name == "CONV":
                    act.wait_ge(front_mm, 7 * n + 3)
                    wait(act, z_mm, KT * n)
                    a(h_rest[:, 1, :], bank, ACT.Identity, bias=conv_b[:, 0:1]).then_inc(conv_ready, 1)
                elif name[:2] == "ZT":
                    act.wait_ge(z_mm, KT * n + j + 1)
                    wait(act, k_mm, G * n)
                    wait(act, v_mm, KT * n)
                    a(z_t[0][:, j, :], bank, ACT.Copy).then_inc(z_hi, 1)
                elif name[0] in "QK":
                    which = "QK".index(name[0])
                    act.wait_ge((q_mm, k_mm)[which], G * n + j + 1)
                    wait(act, (q_stack_in, k_stack_in)[which], 80 * (G * n + j))
                    a(qk_part[0][:, which, :], bank, ACT.Identity, bias=bqk[:, which, j:j + 1]).then_inc(qk_hi_ready, 1)
                elif name[0] == "V":
                    act.wait_ge(v_mm, KT * n + j + 1)
                    wait(act, attn_mm, 16 * (n - 1) + 12 + j + 1)
                    a(v[:, j, :], bank, ACT.Copy).then_inc(v_ready, 1)
                elif name[:2] == "MT":
                    act.wait_ge(shift_mm, G * n + j + 1)
                    wait(act, shift_in, 32 * (G * n + j))
                    a(shift_t[:, :], bank[0:2 * HG * KT, 0:P], ACT.Copy).then_inc(shift_t_ready, 1)

            def raw(n, g):
                if not present(n):
                    return
                act.wait_ge(attn_mm, 16 * n + 4 * g + 4)
                wait(act, attn_ready, G * n + g)
                a(recip[:, :], ps_s[:, :], ACT.Copy)
                wait(act, out_mm, R * n)
                a(attn_t[:, g, :], ps_v[:, :], ACT.Copy).then_inc(raw_ready, 1)

            def stages(b, t):
                if t in Z_SLOT and present(b + 1):
                    z_tiles(b + 1, Z_SLOT.index(t))
                if t == SEL_EXP_SLOT[0] and present(b + 2):
                    sel_exps(b + 2, 0, emb)
                if t == SEL_EXP_SLOT[1] and present(b + 2):
                    act.wait_ge(front_mm, 7 * (b + 2) + 4)
                    sel_exps(b + 2, 1, unit_bank("XCT").rearrange("p (t c) -> p t c", t=KT))
                n = b - 1
                if present(n) and t in NORM_SLOT:
                    r = NORM_SLOT.index(t)
                    act.wait_ge(ln2_pool, LN2_STEPS * (2 * n + r // 2 + 1))
                    wait(act, route_vec, ROUTE_STEPS * (R * n + r - 2) + CHOOSE_STEPS + 1)
                    a(xf[:, r % 2, :], back_h[:, r, :], ACT.Identity, bias=coef[:, r, 3:4],
                      scale=coef[:, r, 2:3]).then_inc(xn_ready, 1)
                    act.wait_ge(xn_ready, R * n + r + 1)
                    a(back_h[:, r, :], back_h[:, r, :], ACT.Identity, bias=coef[:, r, 1:2],
                      scale=coef[:, r, 0:1]).then_inc(base_ready, 1)
                if present(n) and t in SIGN_SLOT:
                    r = SIGN_SLOT.index(t)
                    act.wait_ge(xf_ready, R * n + r + 1)
                    wait(act, route_vec, ROUTE_STEPS * (R * n + r - 2) + 1)
                    a(sign[:, r % 2, :], xf[:, r % 2, :], ACT.Sign).then_inc(sign_ready, 1)

            def batch(b):
                for t in range(SLOTS):
                    if preparing(b, t, 0):
                        prepare()
                    for step in SLOT_STEPS[t]:
                        if step[0] == "S" and present(b):
                            i = step[1]
                            act.wait_ge(score_mm, 64 * b + 4 * t + i + 1)
                            if i == 0:
                                wait(act, attn_mm, 16 * b + t)
                            a(prob[:, i, :], ps_t[:, i % 2, :], ACT.Exp, scale=float(DH) ** -0.5).then_inc(prob_ready, 1)
                        if step == ("S", 3):
                            stages(b, t)
                        if step == ("S", 1) and t % KT == 0:
                            raw(*group_before(b, t // KT))
                        elif step[0] == "E" and present(b + step[2]):
                            unit(b, step[1], b + step[2])

            act.wait_ge(front_in, 16 * FRONT_LOADS)
            run_batches(act, batch)
            act.wait_ge(base_out, 64 * B)
            for n in range(B):
                act.wait_ge(fin_pe, 2 + n)
                a(onehot_t4(n), ps_u[0:NT, n % 2, :], ACT.Copy).then_inc(fin_act, 1)

        @block.vector
        def _(dve):
            vec = nc.vector
            vec.memset(k_stack[SCORE_ROWS:P, :, :, :].bitcast(F32), 1.0).then_inc(setup_vec, 1)
            vec.memset(ones[:, :], 1.0)
            vec.memset(h_emb[:, 0:2], 0.0)
            vec.memset(expo[:, :], -0.5)
            vec.memset(tile_max[:, :], -BIG)
            vec.memset(tile_min[:, :], BIG).then_inc(setup_vec, 1)
            def prepare():
                dve.wait_ge(const_in, 16 * CONST_LOADS)
                vec.reduce_sum(mean_slope[:, :], table[:, 128:256].rearrange("t (j g) -> t j g", g=GRID), X_AXIS).then_inc(setup_vec, 1)
                dve.wait_ge(setup_vec, 3)
                vec.tensor_scalar(tile_sign[:, :], mean_slope[:, :], 0.0, None, ALU.is_lt).then_inc(setup_vec, 1)
                dve.wait_ge(setup_vec, 4)
                vec.scalar_tensor_tensor(tile_sign[:, :], mean_slope[:, :], 0.0, tile_sign[:, :],
                                         ALU.is_gt, ALU.subtract).then_inc(setup_vec, 1)
                dve.wait_ge(sign_bcast, 1)
                vec.tensor_copy(slope_sign[:, :], unit_bank("EX")).then_inc(setup_vec, 1)
                for c in range(KT):
                    last = vec.tensor_scalar(sel[:, c, :], ones[:, :], bv[:, c:c + 1], None, ALU.mult)
                last.then_inc(setup_vec, 1)
                dve.wait_ge(bias_mm, 1)
                vec.tensor_tensor(bout[:, :], unit_bank("EX"), bout[:, :], ALU.add).then_inc(setup_vec, 1)
                for k, (src, dst) in enumerate(((prob, wq), (v, wk), (attn_t, wv))):
                    dve.wait_ge(weight_hi, k + 1)
                    vec.tensor_tensor(dst[1][:, :, :], src[:, :, :], dst[0][:, :, :].bitcast(F32), ALU.subtract).then_inc(weight_lo, 1)
                dve.wait_ge(weight_lo, 3)

            def embed(n):
                dve.wait_ge(rows_in, 64 * (n + 1))
                vec.scalar_tensor_tensor(emb[:, :, :], emb[:, :, :], float(np.sqrt(np.float32(C))), posenc[:, :, :],
                                         ALU.mult, ALU.add).then_inc(emb_ready, 1)

            def chain(n, k, ins):
                ins.then_inc(front_vec, 1)
                dve.wait_ge(front_vec, FRONT_STEPS * n + k)

            def selection_max(n, which, src):
                chain(n, 2 * which + 1, vec.reduce_max(sel_stat[:, 0, :], src, X_AXIS))
                ins = vec.tensor_scalar(sel_stat[:, 1, :], sel_stat[:, 0, :], -1.0, None, ALU.mult)
                ins.then_inc(sel_max, 1)

            def selection_norm(n, which):
                dve.wait_ge(sel_exp, 2 * n + which + 1)
                chain(n, 2 * which + 2, vec.reciprocal(sel_stat[:, 3, :], sel_stat[:, 2, :]))
                vec.tensor_tensor(sel[:, :, :], sel[:, :, :], sel_stat[:, 3, :].unsqueeze(2).to_broadcast([P, KT, C]),
                                  ALU.mult).then_inc(sel_ready, 1)

            def unit(b, name, n):
                bank = unit_bank(name)
                j = int(name[-1]) if name[-1].isdigit() else 0
                if name == "EX":
                    dve.wait_ge(emb_ready, n + 1)
                    selection_max(n, 0, emb[:, :, :])
                elif name == "XCT":
                    dve.wait_ge(front_mm, 7 * n + 4)
                    selection_max(n, 1, bank.rearrange("p (t c) -> p t c", t=KT))
                elif name[:2] == "ZT":
                    dve.wait_ge(z_hi, KT * n + j + 1)
                    vec.tensor_tensor(z_t[1][:, j, :], bank, z_t[0][:, j, :].bitcast(F32), ALU.subtract).then_inc(z_lo, 1)
                elif name[0] in "QK":
                    which = "QK".index(name[0])
                    dve.wait_ge(qk_hi_ready, 8 * n + 2 * j + which + 1)
                    vec.scalar_tensor_tensor(qk_part[1][:, which, :], bank, bqk[:, which, j:j + 1],
                                             qk_part[0][:, which, :].bitcast(F32), ALU.add, ALU.subtract).then_inc(qk_lo_ready, 1)
                elif name[:3] == "OUT":
                    dve.wait_ge(out_mm, R * n + j + 1)
                    dve.wait_ge(bout_added, R * n + R)
                    vec.tensor_tensor(back_h[:, j, :], bank, back_h[:, j, :], ALU.add).then_inc(h2_ready, 1)
                    dve.wait_ge(h2_ready, R * n + j + 1)
                    vec.bn_stats(stats2[:, j, :], back_h[:, j, :]).then_inc(ln2_stats, 1)
                    dve.wait_ge(ln2_stats, 2 * (R * n + j) + 1)
                    wait(dve, ln2_pool, LN2_STEPS * (2 * (n - 1) + j // 2 + 1))
                    apart(dve, dve_carrier)
                    vec.bn_aggr(mv2[:, j, :], stats2[:, j, :]).then_inc(ln2_stats, 1)

            def ln1_first(n):
                dve.wait_ge(h_emb_ready, n + 1)
                dve.wait_ge(conv_ready, n + 1)
                dve.wait_ge(ext_ready, 2 * n + 1)
                for r in range(R - 1):
                    vec.bn_stats(stats1[:, r, :], h_tile(r))

            def ln1_last(n):
                dve.wait_ge(ext_ready, 2 * n + 2)
                chain(n, 5, vec.bn_stats(stats1[:, R - 1, :], h_tile(R - 1)))
                wait(dve, ln1_pool, LN1_STEPS * n)
                apart(dve, dve_carrier)
                for r in range(R):
                    last = vec.bn_aggr(mv1[:, r, :], stats1[:, r, :])
                last.then_inc(ln1_stats, 1)

            def route(n, r):
                first = ROUTE_STEPS * (R * n + r)
                done = [0]

                def step(ins):
                    done[0] += 1
                    ins.then_inc(route_vec, 1)
                    return first + done[0]

                s = sign[:, r % 2, :]
                by_cluster = "p (c t) -> p c t"
                dve.wait_ge(signed_ready, R * n + r + 1)
                yield step(vec.reduce_sum(tile_score[:, :], s.rearrange("p (t j) -> p t j", j=DS), X_AXIS))
                yield step(vec.reduce_sum(cluster_score[:, :], tile_score[:, :].rearrange(by_cluster, t=NT // CL), X_AXIS))
                yield step(vec.scalar_tensor_tensor(cluster_key[:, :], cluster_score[:, :], float(CL), cluster_tie[:, :],
                                                    ALU.mult, ALU.add))
                yield step(vec.scalar_tensor_tensor(tile_key[:, :], tile_score[:, :], float(DS), tile_tie[:, :],
                                                    ALU.mult, ALU.add))
                yield step(vec.scalar_tensor_tensor(key[:, :].rearrange(by_cluster, t=NT // CL),
                                                    cluster_key[:, :].unsqueeze(2).to_broadcast([P, CL, NT // CL]), 256.0,
                                                    tile_key[:, :].rearrange(by_cluster, t=NT // CL), ALU.mult, ALU.add))
                yield step(vec.reduce_max(key_max[:, :], key[:, :], X_AXIS))
                wait(dve, masked, R * n + r - 1)
                yield step(vec.tensor_scalar(onehot[:, r % 2, :], key[:, :], key_max[:, 0:1], None, ALU.is_equal))
                yield step(vec.tensor_tensor(picked[:, :], onehot[:, r % 2, :], iota_tile[:, :], ALU.mult))
                apart(dve, dve_carrier)
                yield step(vec.reduce_sum(tile_idx[:, bass.ds(n, 1), r:r + 1], picked[:, :], X_AXIS))
                assert done[0] == CHOOSE_STEPS

            def pick(n, r):
                first = ROUTE_STEPS * (R * n + r) + CHOOSE_STEPS
                done = [0]

                def step(ins):
                    done[0] += 1
                    ins.then_inc(route_vec, 1)
                    return first + done[0]

                dve.wait_ge(masked, R * n + r + 1)
                oh = onehot[:, r % 2, :]
                apart(dve, dve_carrier)
                yield step(vec.reduce_sum(slices[:, bass.ds(n, 1), r, :], xf[:, r % 2, :].rearrange("p (t j) -> p j t", j=DS), X_AXIS))
                apart(dve, dve_carrier)
                yield step(vec.tensor_reduce(tok_ext[:, 0:1], slices[:, bass.ds(n, 1), r, :], X_AXIS, ALU.max))
                apart(dve, dve_carrier)
                yield step(vec.tensor_reduce(tok_ext[:, 1:2], slices[:, bass.ds(n, 1), r, :], X_AXIS, ALU.min))
                yield step(vec.tensor_scalar(off_mask[:, :], oh, 1.0, BIG, ALU.subtract, ALU.mult))
                yield step(vec.scalar_tensor_tensor(cand[:, :], oh, tok_ext[:, 0:1], off_mask[:, :], ALU.mult, ALU.add))
                yield step(vec.tensor_tensor(tile_max[:, :], tile_max[:, :], cand[:, :], ALU.max))
                yield step(vec.scalar_tensor_tensor(cand[:, :], oh, tok_ext[:, 1:2], off_mask[:, :], ALU.mult, ALU.subtract))
                yield step(vec.tensor_tensor(tile_min[:, :], tile_min[:, :], cand[:, :], ALU.min))
                assert done[0] + CHOOSE_STEPS == ROUTE_STEPS

            def routing(b, t):
                for slot, stage in ((PICK_SLOT, pick), (ROUTE_SLOT, route)):
                    if t in slot and present(b - 1):
                        for count in stage(b - 1, slot.index(t)):
                            yield
                            dve.wait_ge(route_vec, count)

            def batch(b):
                for t in range(SLOTS):
                    g, kt = divmod(t, KT)
                    mn, mg = next_group(b, g)
                    an, ag = group_before(b, g)
                    group = G * mn + mg
                    if t in SEL_NORM_SLOT and present(b + 2):
                        selection_norm(b + 2, SEL_NORM_SLOT.index(t))
                    if kt == KT - 1 and present(mn):
                        dve.wait_ge(max_ready, 16 * group + 16)
                        wait(dve, shift_mm, group)
                        vec.tensor_scalar(shift[:, 0:16], row_max[:, mg % 2, :], -1.0, None, ALU.mult).then_inc(shift_ready, 1)
                        dve.wait_ge(shift_ready, 2 * group + 1)
                        vec.scalar_tensor_tensor(shift[:, 16:32], row_max[:, mg % 2, :], -1.0, shift[:, 0:16].bitcast(F32),
                                                 ALU.mult, ALU.subtract).then_inc(shift_ready, 1)
                    between = routing(b, t)
                    if kt == 0:
                        normed = 0
                    norm_goal = 0 if not present(an) else HG if kt > 0 or ag == G - 1 else HG // 2
                    for step in SLOT_STEPS[t]:
                        if step[0] == "M":
                            mn, mg = next_group(b, g, step[1])
                            if present(mn):
                                k = step[2]
                                dve.wait_ge(max_mm, 64 * mn + 16 * mg + k + 1)
                                if k == 0:
                                    wait(dve, shift_ready, 2 * (G * mn + mg - 1))
                                vec.reduce_max(row_max[:, mg % 2, k:k + 1], ps_m[:, k % 2, :], X_AXIS).then_inc(max_ready, 1)
                        if step[0] == "M" or step == ("S", 3):
                            if normed < norm_goal:
                                if normed == 0:
                                    dve.wait_ge(raw_ready, G * an + ag + 1)
                                cols = slice(normed * P, (normed + 1) * P)
                                vec.reciprocal(recip[:, cols], recip[:, cols]).then_inc(recip_ready, 1)
                                normed += 1
                                if normed == HG:
                                    dve.wait_ge(recip_ready, 16 * an + 4 * ag + 4)
                                    vec.tensor_tensor(attn_t[:, ag, :], attn_t[:, ag, :], recip[:, :], ALU.mult).then_inc(attn_ready, 1)
                            else:
                                next(between, None)
                        elif step[0] == "E" and present(b + step[2]):
                            unit(b, step[1], b + step[2])
                        elif step[0] == "S" or step[0] == "U":
                            next(between, None)
                    assert normed >= norm_goal
                    for _ in between:
                        pass
                    if t == STATS_SLOT[0] and present(b + 2):
                        ln1_first(b + 2)
                    if t == STATS_SLOT[1] and present(b + 1):
                        ln1_last(b + 1)
                    if preparing(b, t, STATS_SLOT[1]):
                        prepare()
                    if t == EMBED_SLOT and present(b + 2):
                        embed(b + 2)

            dve.wait_ge(front_in, 16 * FRONT_LOADS)
            run_batches(dve, batch)

            chain_end = [0]

            def step(ins):
                ins.then_inc(fin_vec, 1)
                chain_end[0] += 1
                dve.wait_ge(fin_vec, chain_end[0])

            for n in range(B):
                if n >= 2:
                    dve.wait_ge(fin_pe, n)
                vec.tensor_tensor(onehots(n), iota_tile[:, :].unsqueeze(1).to_broadcast([P, R, NT]),
                                  tile_idx[:, n, :].unsqueeze(2).to_broadcast([P, R, NT]), ALU.is_equal).then_inc(fin_vec, 1)
                chain_end[0] += 1
            dve.wait_ge(fin_pe, 1)
            vec.reduce_max(table[:, 258:259], ps_m[0:NT, 0, 0:P], X_AXIS)
            step(vec.tensor_reduce(table[:, 257:258], ps_m[0:NT, 1, 0:P], X_AXIS, ALU.min))
            step(vec.tensor_tensor(place[:, :, :], row_base[:, :, :], tile_idx[:, :, :], ALU.add))

            def prepare_tokens(n0, n1):
                rows = slice(n0 * R, n1 * R)
                step(vec.tensor_copy(tok[:, :, rows], (ps_s, ps_v)[n0 // AHEAD % 2][:, 3 * n0 * R:3 * n1 * R].rearrange("p (k c) -> p c k", c=3)))
                low, high = (tok[:, c, rows] for c in (1, 2))
                inv = span[:, rows]
                step(vec.tensor_tensor(inv, high, low, ALU.subtract))
                step(vec.tensor_scalar(inv, inv, 1e-8, None, ALU.add))
                step(vec.reciprocal(inv, inv))
                u = by_row(slices)[:, rows]
                wide = [P, (n1 - n0) * R, DS]
                step(vec.tensor_tensor(u, u, low.unsqueeze(2).to_broadcast(wide), ALU.subtract))
                step(vec.tensor_tensor(u, u, inv.unsqueeze(2).to_broadcast(wide), ALU.mult))
                step(vec.tensor_scalar(u, u, 0.0, float(np.float32(1.0 - 1e-6)), ALU.max, ALU.min))
                step(vec.tensor_scalar(u, u, float(GRID), None, ALU.mult))
                step(vec.tensor_copy(cell_int[:, rows], u))
                step(vec.tensor_copy(cell[:, rows], cell_int[:, rows]))
                step(vec.tensor_tensor(above[:, rows], cell[:, rows], u, ALU.is_gt))
                step(vec.tensor_tensor(cell[:, rows], cell[:, rows], above[:, rows], ALU.subtract))
                step(vec.tensor_tensor(u, u, cell[:, rows], ALU.subtract))

            def by_row(buf):
                return buf[:, :, :, :].rearrange("p b r j -> p (b r) j")

            def count(ins):
                ins.then_inc(fin_vec, 1)
                chain_end[0] += 1
                return chain_end[0]

            masked_at = 0
            for n in range(B + 1):
                if n < B and n % AHEAD == 0:
                    dve.wait_ge(fin_tok, n // AHEAD + 1)
                    prepare_tokens(n, n + AHEAD)
                if n < B:
                    rows = slice(n * R, (n + 1) * R)
                    shape = [P, R, DS, GRID]
                    tab = (ps_t, ps_m)[n % 2][:, :, :].rearrange("p a (h s j g) -> p (a h) s j g", h=2, s=2, g=GRID)
                    w = work(n)
                    dve.wait_ge(fin_tab, n + 1)
                    sloped = count(vec.tensor_tensor(w, tab[:, :, 1], by_row(slices)[:, rows].unsqueeze(3).to_broadcast(shape), ALU.mult))
                    vec.tensor_tensor(mask(n), cell[:, rows].unsqueeze(3).to_broadcast(shape),
                                      iota_grid[:, :].unsqueeze(1).unsqueeze(1).to_broadcast(shape), ALU.is_equal)
                    dve.wait_ge(fin_vec, sloped)
                    based = vec.tensor_tensor(w, w, tab[:, :, 0], ALU.add)
                    based.then_inc(fin_free, 1)
                if n > 0:
                    dve.wait_ge(fin_vec, masked_at)
                    if n > 1:
                        dve.wait_ge(fin_delta, n - 1)
                    summed = count(vec.reduce_sum(grid_val[:, :, :], work(n - 1), X_AXIS))
                if n < B:
                    dve.wait_ge(fin_free, n + 1)
                    masked_now = count(vec.tensor_tensor(w, w, mask(n), ALU.mult))
                if n > 0:
                    dve.wait_ge(fin_vec, summed)
                    last_rows = slice((n - 1) * R, n * R)
                    vec.tensor_tensor(delta[:, n - 1], grid_val[:, :, :], tok[:, 0, last_rows].unsqueeze(2).to_broadcast([P, R, DS]),
                                      ALU.mult).then_inc(fin_delta, 1)
                masked_at = masked_now

        @block.gpsimd
        def _(pool):
            gp = nc.gpsimd

            def gather(n):
                pool.wait_ge(ids_in, 16 * (n + 1))
                if not isinstance(n, int) or n > 0:
                    pool.wait_ge(front_mm, 7 * (n - 1) + 1)
                    pool.wait_ge(sel_exp, 2 * (n - 1) + 1)
                apart(pool, pool_carrier)
                for t in range(KT):
                    gp.indirect_dma_start(out=emb[:, t, :], out_offset=None, in_=io["emb_table"],
                                          in_offset=bass.IndirectOffsetOnAxis(ap=token_ids[:, t:t + 1], axis=0)).then_inc(rows_in, 16)

            def rsqrt(step, dst, src, tmp, width):
                step(gp.tensor_tensor(dst, src, expo[:, 0:width], ALU.pow))
                step(gp.tensor_tensor(tmp, dst, dst, ALU.mult))
                step(gp.tensor_tensor(tmp, tmp, src, ALU.mult))
                apart(pool, pool_carrier)
                step(gp.tensor_scalar(tmp, tmp, -0.5, 1.5, ALU.mult, ALU.add))
                step(gp.tensor_tensor(dst, dst, tmp, ALU.mult))

            def stepper(sem_, first):
                done = [0]

                def step(ins):
                    done[0] += 1
                    ins.then_inc(sem_, 1)
                    pool.wait_ge(sem_, first + done[0])
                return step, done

            def ln1(n):
                pool.wait_ge(ln1_stats, n + 1)
                wait(pool, z_ready, R * n)
                step, done = stepper(ln1_pool, LN1_STEPS * n)
                apart(pool, pool_carrier)
                step(gp.tensor_scalar(scr1[:, 0, :], mv1[:, :, 1], LN_EPS, None, ALU.add))
                rsqrt(step, rstd1[:, :], scr1[:, 0, :], scr1[:, 1, :], R)
                step(gp.tensor_tensor(shift1[:, :], mv1[:, :, 0], rstd1[:, :], ALU.mult))
                apart(pool, pool_carrier)
                step(gp.tensor_scalar(shift1[:, :], shift1[:, :], -1.0, None, ALU.mult))
                assert done[0] == LN1_STEPS

            def ln2(n, pair):
                r = slice(2 * pair, 2 * pair + 2)
                pool.wait_ge(ln2_stats, 2 * (R * n + 2 * pair + 2))
                wait(pool, base_ready, R * (n - 1) + 2 * pair + 2)
                step, done = stepper(ln2_pool, LN2_STEPS * (2 * n + pair))
                mean, var = mv2[:, r, 0], mv2[:, r, 1]
                s, a, tmp, c = (scr2[:, 2 * k:2 * k + 2] for k in range(4))
                apart(pool, pool_carrier)
                step(gp.tensor_scalar(s, var, LN_EPS, None, ALU.add))
                rsqrt(step, a, s, tmp, 2)
                step(gp.tensor_tensor(s, var, a, ALU.mult))
                step(gp.tensor_tensor(s, s, a, ALU.mult))
                apart(pool, pool_carrier)
                step(gp.tensor_scalar(s, s, LN_EPS, None, ALU.add))
                rsqrt(step, c, s, tmp, 2)
                step(gp.tensor_tensor(coef[:, r, 2], a, c, ALU.mult))
                apart(pool, pool_carrier)
                step(gp.tensor_scalar(coef[:, r, 0], a, 1.0, None, ALU.add))
                apart(pool, pool_carrier)
                step(gp.tensor_scalar(tmp, mean, -1.0, None, ALU.mult))
                step(gp.tensor_tensor(coef[:, r, 1], tmp, a, ALU.mult))
                step(gp.tensor_tensor(coef[:, r, 3], tmp, coef[:, r, 2], ALU.mult))
                assert done[0] == LN2_STEPS

            def affine(n, r):
                pool.wait_ge(xn_ready, R * n + r + 1)
                x = xf[:, r % 2, :]
                gp.tensor_tensor(x, x, gamma[:, :], ALU.mult).then_inc(xg_ready, 1)
                pool.wait_ge(xg_ready, R * n + r + 1)
                gp.tensor_tensor(x, x, beta[:, :], ALU.add).then_inc(xf_ready, 1)

            def signed(n, r):
                pool.wait_ge(sign_ready, R * n + r + 1)
                s = sign[:, r % 2, :]
                gp.tensor_tensor(s, s, slope_sign[:, :], ALU.mult).then_inc(signed_ready, 1)

            def mask_xf(n, r):
                pool.wait_ge(route_vec, ROUTE_STEPS * (R * n + r) + CHOOSE_STEPS)
                x = xf[:, r % 2, :].rearrange("p (t j) -> p t j", j=DS)
                gp.tensor_tensor(x, x, onehot[:, r % 2, :].unsqueeze(2).to_broadcast([P, NT, DS]), ALU.mult).then_inc(masked, 1)

            def batch(b):
                for t in range(SLOTS):
                    if t == GATHER_SLOT and present(b + 2):
                        gather(b + 2)
                    if t == LN1_SLOT and present(b + 1):
                        ln1(b + 1)
                    if preparing(b, t, SLOTS - 1):
                        prepare()
                    if present(b - 1):
                        for slot, stage in ((ROUTE_SLOT, mask_xf), (SIGN_SLOT, signed), (NORM_SLOT, affine), (LN2_SLOT, ln2)):
                            if t in slot:
                                stage(b - 1, slot.index(t))
                    if t == RELOAD_SLOT + 1 and present(b):
                        pool.wait_ge(back_in, 64 * (b + 1))
                        for r in range(R):
                            gp.tensor_tensor(back_h[:, r, :], back_h[:, r, :], bout[:, :], ALU.add).then_inc(bout_added, 1)

            def prepare():
                pool.wait_ge(setup_vec, 8)
                pool.wait_ge(const_in, 16 * CONST_LOADS)

            run_batches(pool, batch)

            pool.wait_ge(base_out, 64 * B)
            rows8 = io["out"].rearrange("b s (t j) -> (b s t) j", j=DS)
            for n in range(B):
                pool.wait_ge(fin_delta, n + 1)
                for r in range(R):
                    gp.indirect_dma_start(out=rows8, out_offset=bass.IndirectOffsetOnAxis(ap=place[:, n, r:r + 1], axis=0),
                                          in_=delta[:, n, r, :], in_offset=None, compute_op=ALU.add).then_inc(scattered, 16)


def kernel(**inputs):
    import concourse.bacc as bacc
    from concourse.bass_utils import run_bass_kernel_spmd as run

    f32 = np.float32
    arg = {k: np.ascontiguousarray(a) for k, a in inputs.items()}
    half = C // 2
    depths = np.arange(half, dtype=f32)[None, :] / f32(half)
    angles = np.arange(T, dtype=f32)[:, None] * (f32(1.0) / f32(10000.0) ** depths)
    tiles = np.arange(NT)
    data = {
        "x": arg["x"], "emb_table": arg["L0_tok_emb_table"],
        "conv_w": arg["L0_tok_conv_w"].transpose(2, 1, 0), "conv_b": arg["L0_tok_conv_b"],
        "spos0": arg["L0_tok_spos0"], "spos1": arg["L0_tok_spos1"],
        "WqT": arg["L0_attn_Wq"].T, "WkT": arg["L0_attn_Wk"].T, "WvT": arg["L0_attn_Wv"].T, "WoT": arg["L0_attn_Wout"].T,
        "bq": arg["L0_attn_bq"].reshape(G, P).T, "bk": arg["L0_attn_bk"].reshape(G, P).T, "bv": arg["L0_attn_bv"].reshape(KT, P).T, "bout": arg["L0_attn_bout"],
        "gamma": arg["L0_ffn_ln_gamma"], "beta": arg["L0_ffn_ln_beta"],
        "bases": arg["L0_ffn_spline_bases"], "slopes": arg["L0_ffn_spline_slopes"], "oscale": arg["L0_ffn_output_scale"],
        "posenc": np.concatenate([np.sin(angles), np.cos(angles)], axis=-1).astype(f32),
        "ident": np.eye(P, dtype=f32),
        "iota_tile": tiles.astype(f32), "tile_tie": (NT // CL - 1 - tiles % (NT // CL)).astype(f32),
        "cluster_tie": (CL - 1 - np.arange(CL)).astype(f32), "iota_grid": np.arange(GRID).astype(f32),
        "row_base": (NT * (np.arange(B)[None, :, None] * R * P + np.arange(R)[None, None, :] * P
                           + np.arange(P)[:, None, None])).astype(f32),
    }
    nc = bacc.Bacc("TRN2", target_bir_lowering=False, num_devices=1, dynamic_dma_scratch_size=3072)
    arrays, io = {}, {}
    for name, a in data.items():
        a = np.ascontiguousarray(a)
        arrays[f"in_{name}"] = a
        io[name] = nc.dram_tensor(f"in_{name}", a.shape, mybir.dt.from_np(a.dtype), kind="ExternalInput").ap()
    io["out"] = nc.dram_tensor("out_h", (B, R * P, T), F32, kind="ExternalOutput").ap()
    build(nc, io)
    return run(nc, [arrays], core_ids=[0]).results[0]["out_h"]
```
